# Optimizing a Trainium2 kernel written in Bass

```python
import numpy as np
import jax
import jax.numpy as jnp

def _softmax(x, axis=-1):
    return jax.nn.softmax(x, axis=axis)

def _gelu(x):
    return jax.nn.gelu(x, approximate=True)

def _silu(x):
    return jax.nn.silu(x)

def _sigmoid(x):
    return jax.nn.sigmoid(x)

def _layernorm(x, axis=-1, eps=1e-05):
    m = jnp.mean(x, axis=axis, keepdims=True)
    v = jnp.var(x, axis=axis, keepdims=True)
    return (x - m) / jnp.sqrt(v + eps)

def _scatter_add(tgt, idx, src, axis=0):
    return tgt.at[idx].add(src)

def _segment_sum(src, seg, n):
    return jax.ops.segment_sum(src, seg, n)
kernel_name = 'mk_macaron_d1_jaxref_r4_709d52'

def setup_inputs(seed: int=0):
    np.random.seed(seed)
    _w = jnp.asarray

    def _L0_attn_setup():
        import jax, jax.numpy as jnp
        import numpy as np
        HIDDEN = 512
        NUM_HEADS = 6
        HEAD_V = 128
        VALUE_DIM = NUM_HEADS * HEAD_V
        CONV_K = 4
        PHASE_BASE = 10000.0
        EPS = 1e-05

        def _causal_depthwise_conv(x, w):
            B, T, C = x.shape
            K = w.shape[1]
            xp = jnp.pad(x, ((0, 0), (K - 1, 0), (0, 0)))
            y = jnp.zeros_like(x)
            for j in range(K):
                y = y + xp[:, j:j + T, :] * w[:, j]
            return y

        def _rotate(x, ang):
            cos = jnp.cos(ang)
            sin = jnp.sin(ang)
            xe = x[..., ::2]
            xo = x[..., 1::2]
            ye = xe * cos - xo * sin
            yo = xo * cos + xe * sin
            return jnp.stack([ye, yo], axis=-1).reshape(x.shape)

        def _forward(hidden_states, Wq, Wk, Wv, Wa, Wb, Wg, Wo, conv_q, conv_k, conv_v, rms_w):
            B, T, _ = hidden_states.shape
            H, D = (NUM_HEADS, HEAD_V)
            inv_freq = 1.0 / PHASE_BASE ** (jnp.arange(0, D, 2, dtype=jnp.float32) / D)
            q = _causal_depthwise_conv(hidden_states @ Wq, conv_q).reshape(B, T, H, D)
            k = _causal_depthwise_conv(hidden_states @ Wk, conv_k).reshape(B, T, H, D)
            v = _causal_depthwise_conv(hidden_states @ Wv, conv_v).reshape(B, T, H, D)
            theta = q[..., ::2] * inv_freq
            psi = k[..., ::2] * inv_freq
            phi = theta - jnp.concatenate([jnp.zeros_like(theta[:, :1]), theta[:, :-1]], axis=1)
            alpha = jax.nn.sigmoid(hidden_states @ Wa)
            beta = jax.nn.sigmoid(hidden_states @ Wb)
            tm = lambda a: jnp.moveaxis(a, 1, 0)
            xs = (tm(theta), tm(psi), tm(phi), tm(v), tm(alpha), tm(beta))

            def step(state, inp):
                th, ps, ph, vt, at, bt = inp
                retained = _rotate(state, ph) * at[..., None]
                write = _rotate(vt, ps)
                new_state = retained + bt[..., None] * write
                out_t = _rotate(new_state, -th)
                return (new_state, out_t)
            state0 = jnp.zeros((B, H, D), hidden_states.dtype)
            _, out = jax.lax.scan(step, state0, xs)
            out = jnp.moveaxis(out, 0, 1)
            g = (hidden_states @ Wg).reshape(B, T, H, D)
            rms = jax.lax.rsqrt(jnp.mean(jnp.square(out), axis=-1, keepdims=True) + EPS)
            o = out * rms * rms_w * jax.nn.silu(g)
            return o.reshape(B, T, VALUE_DIM) @ Wo
        key = jax.random.key(seed)
        ks = jax.random.split(key, 12)
        s = 0.02
        return {'hidden_states': jax.random.normal(ks[0], (2, 512, HIDDEN), jnp.float32), 'Wq': jax.random.normal(ks[1], (HIDDEN, VALUE_DIM), jnp.float32) * s, 'Wk': jax.random.normal(ks[2], (HIDDEN, VALUE_DIM), jnp.float32) * s, 'Wv': jax.random.normal(ks[3], (HIDDEN, VALUE_DIM), jnp.float32) * s, 'Wa': jax.random.normal(ks[4], (HIDDEN, NUM_HEADS), jnp.float32) * s, 'Wb': jax.random.normal(ks[5], (HIDDEN, NUM_HEADS), jnp.float32) * s, 'Wg': jax.random.normal(ks[6], (HIDDEN, VALUE_DIM), jnp.float32) * s, 'Wo': jax.random.normal(ks[7], (VALUE_DIM, HIDDEN), jnp.float32) * s, 'conv_q': jax.random.normal(ks[8], (VALUE_DIM, CONV_K), jnp.float32) * s, 'conv_k': jax.random.normal(ks[9], (VALUE_DIM, CONV_K), jnp.float32) * s, 'conv_v': jax.random.normal(ks[10], (VALUE_DIM, CONV_K), jnp.float32) * s, 'rms_w': jnp.ones((HEAD_V,), jnp.float32)}
    _L0_attn_in = _L0_attn_setup()

    def _L0_ffn_setup():
        import jax, jax.numpy as jnp
        import numpy as np
        E, TOP_K, D, H = (8, 2, 512, 352)
        B, S = (2, 512)
        key = jax.random.key(seed)
        ks = jax.random.split(key, 8)
        x = jax.random.normal(ks[0], (B, S, D), dtype=jnp.float32)
        gate_w = jax.random.normal(ks[1], (E, D), dtype=jnp.float32) * (1.0 / np.sqrt(D))
        gate_b = jax.random.normal(ks[2], (E,), dtype=jnp.float32) * 0.01
        bias = jnp.zeros((E,), dtype=jnp.float32)
        w1 = jax.random.normal(ks[3], (E, H, D), dtype=jnp.float32) * (1.0 / np.sqrt(D))
        b1 = jax.random.normal(ks[4], (E, H), dtype=jnp.float32) * 0.01
        w2 = jax.random.normal(ks[5], (E, D, H), dtype=jnp.float32) * (1.0 / np.sqrt(H))
        b2 = jax.random.normal(ks[6], (E, D), dtype=jnp.float32) * 0.01
        return {'x': x, 'gate_w': gate_w, 'gate_b': gate_b, 'bias': bias, 'w1': w1, 'b1': b1, 'w2': w2, 'b2': b2}
    _L0_ffn_in = _L0_ffn_setup()
    _d = {'L0_attn_hidden_states': _L0_attn_in['hidden_states'], 'L0_attn_Wq': _L0_attn_in['Wq'], 'L0_attn_Wk': _L0_attn_in['Wk'], 'L0_attn_Wv': _L0_attn_in['Wv'], 'L0_attn_Wa': _L0_attn_in['Wa'], 'L0_attn_Wb': _L0_attn_in['Wb'], 'L0_attn_Wg': _L0_attn_in['Wg'], 'L0_attn_Wo': _L0_attn_in['Wo'], 'L0_attn_conv_q': _L0_attn_in['conv_q'], 'L0_attn_conv_k': _L0_attn_in['conv_k'], 'L0_attn_conv_v': _L0_attn_in['conv_v'], 'L0_attn_rms_w': _L0_attn_in['rms_w'], 'L0_ffn_gate_w': _L0_ffn_in['gate_w'], 'L0_ffn_gate_b': _L0_ffn_in['gate_b'], 'L0_ffn_bias': _L0_ffn_in['bias'], 'L0_ffn_w1': _L0_ffn_in['w1'], 'L0_ffn_b1': _L0_ffn_in['b1'], 'L0_ffn_w2': _L0_ffn_in['w2'], 'L0_ffn_b2': _L0_ffn_in['b2']}
    _x0 = _d['L0_attn_hidden_states']
    _d['L0_attn_hidden_states'] = jax.random.normal(jax.random.fold_in(jax.random.key(seed), 1), (1, 2048, 512), dtype=_x0.dtype)
    del _x0
    return _d

def reference(L0_attn_hidden_states, L0_attn_Wq, L0_attn_Wk, L0_attn_Wv, L0_attn_Wa, L0_attn_Wb, L0_attn_Wg, L0_attn_Wo, L0_attn_conv_q, L0_attn_conv_k, L0_attn_conv_v, L0_attn_rms_w, L0_ffn_gate_w, L0_ffn_gate_b, L0_ffn_bias, L0_ffn_w1, L0_ffn_b1, L0_ffn_w2, L0_ffn_b2):

    def _L0_attn_ref(hidden_states, Wq, Wk, Wv, Wa, Wb, Wg, Wo, conv_q, conv_k, conv_v, rms_w):
        import jax, jax.numpy as jnp
        import numpy as np
        HIDDEN = 512
        NUM_HEADS = 6
        HEAD_V = 128
        VALUE_DIM = NUM_HEADS * HEAD_V
        CONV_K = 4
        PHASE_BASE = 10000.0
        EPS = 1e-05

        def _causal_depthwise_conv(x, w):
            B, T, C = x.shape
            K = w.shape[1]
            xp = jnp.pad(x, ((0, 0), (K - 1, 0), (0, 0)))
            y = jnp.zeros_like(x)
            for j in range(K):
                y = y + xp[:, j:j + T, :] * w[:, j]
            return y

        def _rotate(x, ang):
            cos = jnp.cos(ang)
            sin = jnp.sin(ang)
            xe = x[..., ::2]
            xo = x[..., 1::2]
            ye = xe * cos - xo * sin
            yo = xo * cos + xe * sin
            return jnp.stack([ye, yo], axis=-1).reshape(x.shape)

        def _forward(hidden_states, Wq, Wk, Wv, Wa, Wb, Wg, Wo, conv_q, conv_k, conv_v, rms_w):
            B, T, _ = hidden_states.shape
            H, D = (NUM_HEADS, HEAD_V)
            inv_freq = 1.0 / PHASE_BASE ** (jnp.arange(0, D, 2, dtype=jnp.float32) / D)
            q = _causal_depthwise_conv(hidden_states @ Wq, conv_q).reshape(B, T, H, D)
            k = _causal_depthwise_conv(hidden_states @ Wk, conv_k).reshape(B, T, H, D)
            v = _causal_depthwise_conv(hidden_states @ Wv, conv_v).reshape(B, T, H, D)
            theta = q[..., ::2] * inv_freq
            psi = k[..., ::2] * inv_freq
            phi = theta - jnp.concatenate([jnp.zeros_like(theta[:, :1]), theta[:, :-1]], axis=1)
            alpha = jax.nn.sigmoid(hidden_states @ Wa)
            beta = jax.nn.sigmoid(hidden_states @ Wb)
            tm = lambda a: jnp.moveaxis(a, 1, 0)
            xs = (tm(theta), tm(psi), tm(phi), tm(v), tm(alpha), tm(beta))

            def step(state, inp):
                th, ps, ph, vt, at, bt = inp
                retained = _rotate(state, ph) * at[..., None]
                write = _rotate(vt, ps)
                new_state = retained + bt[..., None] * write
                out_t = _rotate(new_state, -th)
                return (new_state, out_t)
            state0 = jnp.zeros((B, H, D), hidden_states.dtype)
            _, out = jax.lax.scan(step, state0, xs)
            out = jnp.moveaxis(out, 0, 1)
            g = (hidden_states @ Wg).reshape(B, T, H, D)
            rms = jax.lax.rsqrt(jnp.mean(jnp.square(out), axis=-1, keepdims=True) + EPS)
            o = out * rms * rms_w * jax.nn.silu(g)
            return o.reshape(B, T, VALUE_DIM) @ Wo
        return _forward(hidden_states, Wq, Wk, Wv, Wa, Wb, Wg, Wo, conv_q, conv_k, conv_v, rms_w)

    def _L0_ffn_ref(x, gate_w, gate_b, bias, w1, b1, w2, b2):
        import jax, jax.numpy as jnp
        import numpy as np
        E, TOP_K, D, H = (8, 2, 512, 352)
        B, S = (2, 512)
        b, s, d = x.shape
        xf = x.reshape(-1, d)
        scores = xf @ gate_w.T + gate_b + bias
        top_scores, top_idx = jax.lax.top_k(scores, TOP_K)
        gates = jax.nn.softmax(top_scores, axis=-1)
        comb = jnp.sum(jax.nn.one_hot(top_idx, E, dtype=gates.dtype) * gates[..., None], axis=1)
        h = jax.nn.silu(jnp.einsum('td,ehd->teh', xf, w1) + b1)
        y = jnp.einsum('teh,edh->ted', h, w2) + b2
        out = jnp.einsum('ted,te->td', y, comb)
        return out.reshape(b, s, d)
    x = L0_attn_hidden_states
    x = x + 0.5 * _L0_ffn_ref(_layernorm(x, axis=-1), L0_ffn_gate_w, L0_ffn_gate_b, L0_ffn_bias, L0_ffn_w1, L0_ffn_b1, L0_ffn_w2, L0_ffn_b2)
    x = x + _L0_attn_ref(_layernorm(x, axis=-1), L0_attn_Wq, L0_attn_Wk, L0_attn_Wv, L0_attn_Wa, L0_attn_Wb, L0_attn_Wg, L0_attn_Wo, L0_attn_conv_q, L0_attn_conv_k, L0_attn_conv_v, L0_attn_rms_w)
    x = x + 0.5 * _L0_ffn_ref(_layernorm(x, axis=-1), L0_ffn_gate_w, L0_ffn_gate_b, L0_ffn_bias, L0_ffn_w1, L0_ffn_b1, L0_ffn_w2, L0_ffn_b2)
    return x

_drawn_inputs = setup_inputs


def setup_inputs(seed=0):
    import zlib

    import numpy as np

    out = dict(_drawn_inputs(seed))
    spreads = {'L0_attn_rms_w': (1.0, 0.2), 'L0_ffn_bias': (0.0, 0.1)}
    factors = {'L0_attn_Wq': 8.0,
     'L0_attn_Wk': 8.0,
     'L0_attn_Wa': 2.897,
     'L0_attn_conv_q': 8.0,
     'L0_attn_conv_k': 8.0,
     'L0_ffn_gate_b': 2.91,
     'L0_ffn_b1': 7.018,
     'L0_ffn_b2': 5.062}
    for name, (base, spread) in spreads.items():
        noise = np.random.default_rng([zlib.crc32(name.encode()), seed]).standard_normal(out[name].shape)
        drawn = base * np.exp(spread * noise) if base else spread * noise
        out[name] = jnp.asarray(drawn.astype(out[name].dtype))
    for name, factor in factors.items():
        out[name] = (out[name] * factor).astype(out[name].dtype)
    return out
```

```python
from contextlib import ExitStack

import numpy as np

import concourse.bass as bass
from concourse import mybir

F32, F16, I32 = mybir.dt.float32, mybir.dt.float16, mybir.dt.int32
ACT = mybir.ActivationFunctionType
ALU = mybir.AluOpType
AX = mybir.AxisListType.X

P = 128
T, D = 2048, 512
E, HID = 8, 352
NT = T // P
KD = D // P
KH = 3
LAST = HID - 2 * P
SLOT_TILES = (2 * T + E * (P - 1)) // P
FW = KD * HID + KH * D
HEADS = 6
PAIRS = HEADS // 2
KINDS = 6
TAPS = 4
CH = 512
NCH = T // CH
TPC = CH // P
HALO = TAPS - 1
NCOL = PAIRS * KINDS * P
NAB = 2 * HEADS
AW = KD * NCOL + KD * NAB + 2 * PAIRS * D
AB0, WO0 = KD * NCOL, KD * NCOL + KD * NAB
PIECES = 12
PIECE = AW // PIECES
WSCALE = 256.0
UNSCALE = 1.0 / WSCALE
EPS = 1e-5
MAGIC = 12582912.0
RSQRT_SEED = float(0x5F3759DF)
PI2 = float(2 * np.pi)
CHUNK_STEPS = 123


class Chain:

    def __init__(self, eng, sem):
        self.eng, self.sem, self.base, self.n = eng, sem, 0, 0

    def __call__(self, ins):
        self.n += 1
        ins.then_inc(self.sem, 1)
        return self.n

    def wait(self, token=None):
        self.eng.wait_ge(self.sem, self.base + (self.n if token is None else token))

    def loop(self, lo, hi, per, body):
        start, self.n = self.base + self.n, 0
        with self.eng.Fori(lo, hi) as i:
            self.base = start + (i - lo) * per
            body(i)
            assert self.n == per, (self.n, per)
        self.base, self.n = start + (hi - lo) * per, 0


def build(nc, x_in, ffn_w, gate_wT, gate_bias, b1, att_w, conv, rms_w, turns, out):
    ctx = ExitStack()
    with ctx:
        def sb(name, shape, dt=F32):
            return ctx.enter_context(nc.sbuf_tensor(name, shape, dt))

        def sem(name):
            return ctx.enter_context(nc.semaphore(name))

        def dram(name, shape, dt=F32):
            return nc.dram_tensor(name, shape, dt).ap()

        xn_rows = dram("xn_rows", (T, D))
        slot_out = dram("slot_out", (SLOT_TILES * P, D))
        x1_rows = dram("x1_rows", (T, D))
        x2_rows = dram("x2_rows", (T, D))
        w_saved = dram("w_saved", (E, P, 2 * FW), F16)

        att = sb("att", [P, 2, AW], F16)
        ident = sb("ident", [P, P])
        ones = sb("ones", [P, P])
        before = sb("before", [P, P])
        headmean = sb("headmean", [P, P])
        sel = sb("sel", [44, 2, PAIRS, P], F16)
        desc = sb("desc", [P, NT, E])
        lane = sb("lane", [P, P])
        tokid = sb("tokid", [P, NT])
        restart = sb("restart", [P, E, NT])
        half_pi = sb("half_pi", [P, 1])
        epsc = sb("epsc", [P, 1])
        conv_sb = sb("conv_sb", [P, PAIRS, 4, TAPS])
        cang = sb("cang", [P, PAIRS, 2, TAPS])
        rms_sb = sb("rms_sb", [P, 2])
        turns_sb = sb("turns_sb", [P, 2])
        gw = sb("gw", [P, KD, E])
        gb = sb("gb", [P, 2, E])
        pos_i = sb("pos_i", [P, 2, NT], I32)
        ghalf = sb("ghalf", [P, 2, NT])
        slot_tok = sb("slot_tok", [P, SLOT_TILES], I32)
        tile_exp = sb("tile_exp", [P, SLOT_TILES], I32)
        cur = sb("cur", [P, 4, 2], I32)
        mv = sb("mv", [P, TPC, 2])
        bst = sb("bst", [P, TPC, 6])
        nt4 = sb("nt4", [P, 4, TPC])
        rstd = sb("rstd", [P, 2, 2, TPC])

        ARENA = 38800
        arena = sb("arena", [P, ARENA])

        class Layout:
            def __init__(self, at=0):
                self.at = at

            def __call__(self, shape, dt=F32, rows=P):
                n = int(np.prod(shape))
                words = n if dt != F16 else (n + 1) // 2
                v = arena[0:rows, self.at:self.at + words]
                self.at += words
                assert self.at <= ARENA, self.at
                if dt != F32:
                    v = v.bitcast(dt)
                if len(shape) > 1:
                    names = " ".join("abcd"[:len(shape)])
                    v = v.rearrange(f"p ({names}) -> p {names}", **dict(zip("abcd", shape)))
                return v

        lay = Layout()
        wexp = lay([E, 2 * FW], F16)
        wflat = arena[:, 0:E * FW].bitcast(F16)
        b1_bc = lay([E * HID])
        moe_at = lay.at
        xg = lay([2, D])
        xh, xl = lay([2, D], F16), lay([2, D], F16)
        z = lay([2, HID])
        hact = lay([2, KH * P])
        hh, hl = lay([2, KH, P], F16), lay([2, KH, P], F16)
        yo = lay([2, D])
        lay2 = Layout(moe_at)
        lg = lay2([2, TPC, D])
        xnT = lay2([2, KD, P])
        lay = Layout(max(lay.at, lay2.at))
        fin_at = lay.at
        S, S2, OH1, OH2, KEY, M8, QP = (lay([NT, E]) for _ in range(7))
        CE, SC, EX = (lay([E, NT]) for _ in range(3))
        m1, m2, k1, dm, th = (lay([NT]) for _ in range(5))
        posf, hi_f, lo_f = (lay([2, NT]) for _ in range(3))
        tl, en, st8, base8, one8 = (lay([E]) for _ in range(5))
        cmp = lay([SLOT_TILES, E])
        evf = lay([SLOT_TILES])
        oh_at = lay.at
        OHlo = lay([2, NT, P], F16)
        OHhi = lay([2, NT, SLOT_TILES + 1], F16)
        stage_at = Layout(oh_at)
        apiece = stage_at([PIECE])
        wstage = att[:, :, 0:2 * FW].bitcast(F32)

        lay = Layout()
        raw = lay([PAIRS, 4, CH + HALO])
        xgrp = lay([TPC, D])
        yg = lay([TPC, 2, D])
        xnt = lay([2, D])
        xTh, xTl = lay([KD, CH], F16), lay([KD, CH], F16)
        abt, abs_ = lay([CH], rows=44), lay([CH], rows=44)
        sigab = lay([CH], F16, rows=44)
        sg = lay([PAIRS, 2, CH])
        ang, rnd, frac, sn, af, cs = (lay([CH]) for _ in range(6))
        vcon = lay([2, CH])
        tmp = lay([4, CH])
        res = lay([PAIRS, 2, CH])
        carry = lay([PAIRS, 2])
        sqs = lay([2, CH])
        sqa = lay([CH])
        rt, ri = lay([CH]), lay([CH])
        on = lay([2, CH])
        oh, ol = lay([2 * PAIRS, CH], F16), lay([2 * PAIRS, CH], F16)
        ob = lay([2, D])
        x1t = lay([2, D])
        x2t = lay([2, D])

        bank = [ctx.enter_context(nc.psum_tensor(f"bank{i}", [P, 512], F32)) for i in range(8)]

        def w1(part, k, ev):
            return wflat[:, bass.ds(ev * (2 * FW) + (part * FW + k * HID), HID)]

        def w2(part, c, ev):
            return wflat[:, bass.ds(ev * (2 * FW) + (part * FW + KD * HID + c * D), D)]

        consts = sem("consts")
        params = sem("params")
        b1_in = [sem("b1_in"), sem("b1_back")]
        w_in = [sem("w_in0"), sem("w_in1")]
        w_hi = sem("w_hi")
        w_ready = sem("w_ready")
        w_save = sem("w_save")
        w_back = sem("w_back")
        a_in = sem("a_in")
        a_hi, a_lo = sem("a_hi"), sem("a_lo")
        g_in = [sem("g_in0"), sem("g_in1")]
        s_rstd = sem("s_rstd")
        s_xn = sem("s_xn")
        g_out = [sem("g_out0"), sem("g_out1")]
        s_xt = sem("s_xt")
        s_xtc = sem("s_xtc")
        s_gate = sem("s_gate")
        s_onehot = sem("s_onehot")
        s_dm = sem("s_dm")
        s_tanh = sem("s_tanh")
        s_count = sem("s_count")
        s_ohs = sem("s_ohs")
        s_inv = sem("s_inv")
        s_route = sem("s_route")
        s_cur = sem("s_cur")
        xg_in = [sem("xg_in0"), sem("xg_in1")]
        m_xt, m_z, m_ht, m_y = (sem(n) for n in ("m_xt", "m_z", "m_ht", "m_y"))
        m_xh, m_h, m_hh = (sem(n) for n in ("m_xh", "m_h", "m_hh"))
        m_xl, m_zb, m_hl, m_yo = (sem(n) for n in ("m_xl", "m_zb", "m_hl", "m_yo"))
        m_yst = [sem("m_yst0"), sem("m_yst1")]
        dve = sem("dve")
        pool = sem("pool")
        actc = sem("actc")
        cg_in = sem("cg_in")
        yg_in = [sem(f"yg_in{i}") for i in range(4)]
        c_comb = sem("c_comb")
        x1_st = sem("x1_st")
        c_rstd, c_xn, c_xt, c_xh, c_xl = (sem(n) for n in ("c_rstd", "c_xn", "c_xt", "c_xh", "c_xl"))
        c_ab, c_th, c_sig, c_sgh, c_sgl = (sem(n) for n in ("c_ab", "c_th", "c_sig", "c_sgh", "c_sgl"))
        c_proj, c_ev, c_frac, c_trig, c_conv = (sem(n) for n in ("c_proj", "c_ev", "c_frac", "c_trig", "c_conv"))
        c_bc, c_scan, c_sq, c_sqa, c_ssq, c_rt = (sem(n) for n in ("c_bc", "c_scan", "c_sq", "c_sqa", "c_ssq", "c_rt"))
        c_norm, c_out, c_ob, c_x2 = (sem(n) for n in ("c_norm", "c_out", "c_ob", "c_x2"))
        x1t_in = [sem("x1t_in0"), sem("x1t_in1")]
        x2_st = [sem("x2_st0"), sem("x2_st1")]
        f_in, f_out, f_comb = sem("f_in"), sem("f_out"), sem("f_comb")
        zero_init = sem("zero_init")

        block = ctx.enter_context(nc.Block())

        def rows4(ap, g):
            return ap[bass.ds(g * CH, CH), :].rearrange("(a p) d -> p a d", p=P)

        @block.sync
        def _(sp):
            for dst, src in ((gw[:, :, :], gate_wT.rearrange("(k p) e -> p k e", p=P)),
                             (gb[:, :, :], gate_bias.partition_broadcast(P)),
                             (conv_sb[:, :, :, :], conv), (rms_sb[:, :], rms_w), (turns_sb[:, :], turns)):
                sp.dma_start(dst, src).then_inc(params, 16)
            for par in (0, 1):
                sp.sem_inc(g_out[par], 1)
                sp.sem_inc(m_yst[par], 1)
                sp.sem_inc(x2_st[par], 1)

            def norm_groups(src, ph):
                def fetch(g):
                    par, j = g % 2, g // 2
                    sp.wait_ge(g_out[par], 16 * (2 * ph + j) + 1)
                    if g > 1:
                        sp.wait_ge(s_xt, NT * ph + TPC * (g - 1))
                    sp.dma_start(lg[:, par], rows4(src, g)).then_inc(g_in[par], 16)

                def put(g):
                    sp.wait_ge(s_xn, NT * ph + TPC * (g + 1))
                    sp.dma_start(rows4(xn_rows, g), lg[:, g % 2]).then_inc(g_out[g % 2], 16)

                fetch(0)
                fetch(1)
                for g in range(NCH):
                    put(g)
                    if g + 2 < NCH:
                        fetch(g + 2)

            def slots(ph):
                def store(t, par):
                    sp.wait_ge(m_yo, SLOT_TILES * ph + t + 3)
                    sp.dma_start(slot_out[bass.ds(t * P, P), :], yo[:, par]).then_inc(m_yst[par], 16)

                def turn(j, pieces):
                    if pieces:
                        sp.wait_ge(a_lo, j + 1)
                        sp.dma_start(apiece, att_w[:, bass.ds(j * PIECE, PIECE)]).then_inc(a_in, 16)
                    store(2 * j, 0)
                    store(2 * j + 1, 1)

                split = 0 if ph else PIECES
                if split:
                    sp.wait_ge(s_inv, 1)
                    with sp.Fori(0, split) as j:
                        turn(j, True)
                with sp.Fori(split, SLOT_TILES // 2) as j:
                    turn(j, False)
                store(SLOT_TILES - 1, 0)

            def outputs_stored(ph):
                for par in (0, 1):
                    sp.wait_ge(m_yst[par], 16 * (ph + 1) * (SLOT_TILES // 2 + 1 - par) + 1)

            norm_groups(x_in, 0)
            slots(0)
            outputs_stored(0)

            def group_in(c):
                sp.dma_start(xgrp, rows4(x_in, c)).then_inc(cg_in, 16)

            def group_out(c):
                sp.wait_ge(c_comb, TPC * (c + 1))
                sp.dma_start(rows4(x1_rows, c), xgrp).then_inc(x1_st, 16)

            def next_group_in(c):
                sp.wait_ge(x1_st, 16 * c)
                sp.wait_ge(c_xn, TPC * c)
                group_in(c)

            def out_tiles(c):
                def fetch(i):
                    n = TPC * c + i
                    sp.wait_ge(c_x2, n + 1)
                    sp.dma_start(x1t[:, i % 2], x1_rows[bass.ds(n * P, P), :]).then_inc(x1t_in[i % 2], 16)

                def put(i):
                    n = TPC * c + i
                    sp.wait_ge(c_x2, n + 3)
                    sp.dma_start(x2_rows[bass.ds(n * P, P), :], x2t[:, i % 2]).then_inc(x2_st[i % 2], 16)

                fetch(0)
                fetch(1)
                for i in range(TPC):
                    put(i)
                    if i + 2 < TPC:
                        fetch(i + 2)

            sp.wait_ge(w_save, 16)
            group_in(0)
            group_out(0)
            next_group_in(1)
            group_out(1)
            for c in range(1, NCH - 1):
                next_group_in(c + 1)
                out_tiles(c - 1)
                group_out(c + 1)
            out_tiles(NCH - 2)
            sp.wait_ge(x1_st, 16 * NCH)
            out_tiles(NCH - 1)
            for par in (0, 1):
                sp.wait_ge(x2_st[par], 16 * (NT // 2) + 1)

            norm_groups(x2_rows, 1)
            sp.dma_start(wexp, w_saved.rearrange("e p w -> p e w")).then_inc(w_back, 16)
            sp.dma_start(b1_bc, b1.partition_broadcast(P)).then_inc(b1_in[1], 16)
            slots(1)
            outputs_stored(1)

            for g in range(NCH):
                if g:
                    sp.wait_ge(f_out, 16 * g)
                sp.dma_start(xgrp, rows4(x2_rows, g)).then_inc(f_in, 16)
                sp.wait_ge(f_comb, TPC * (g + 1))
                sp.dma_start(rows4(out, g), xgrp).then_inc(f_out, 16)
            sp.wait_ge(f_out, 16 * NCH)

        @block.gpsimd
        def _(gp):
            ch = Chain(gp, pool)

            def seq(ins):
                ch(ins)
                ch.wait()

            def select(out_, in_, op, fill, base, pattern, per_row):
                seq(gp.affine_select(out=out_, in_=in_, compare_op=op, fill=fill, base=base, pattern=pattern,
                                     channel_multiplier=per_row))

            def count(out_, base, pattern, per_row):
                return gp.iota(out_, pattern=pattern, base=base, channel_multiplier=per_row,
                               allow_small_or_imprecise_dtypes=True)

            for buf, value in ((ident, 0.0), (ones, 1.0), (headmean, 1.0 / P), (sel, 0.0),
                               (half_pi, PI2 / 4), (epsc, EPS), (restart, 1.0)):
                seq(gp.memset(buf.ap(), value))
            seq(gp.memset(restart[:, :, 0:1], 0.0))
            seq(gp.memset(headmean[0:64, 64:128], 0.0))
            seq(gp.memset(headmean[64:128, 0:64], 0.0))
            select(ident[:, :], ident[:, :], ALU.not_equal, 1.0, 0, [[-1, P]], 1)
            select(before[:, :], ones[:, :], ALU.is_gt, 0.0, 0, [[1, P]], -1)
            sel_rows = sel[:, :, :, :].rearrange("r t p (h c) -> r (t p h) c", h=2)
            for first in (0, 32):
                select(sel_rows, sel_rows, ALU.not_equal, 1.0, -first, [[-1, NAB], [0, 64]], 1)
            seq(count(desc[:, :, :], E, [[0, NT], [-1, E]], 0))
            seq(count(lane[:, :], 0, [[1, P]], 0))
            count(tokid[:, :], 0, [[P, NT]], 1).then_inc(consts, 1)
            gp.wait_ge(consts, 1)
            gp.dma_start(b1_bc, b1.partition_broadcast(P)).then_inc(b1_in[0], 16)
            with gp.Fori(0, E // 2) as j:
                for par in (0, 1):
                    e = 2 * j + par
                    gp.wait_ge(w_ready, e + 1)
                    gp.dma_start(wstage[:, par], ffn_w[bass.ds(e, 1), :, :].rearrange("a p w -> p (a w)")).then_inc(w_in[par], 16)
            gp.wait_ge(w_ready, E + 2)
            gp.dma_start(w_saved.rearrange("e p w -> p e w"), wexp).then_inc(w_save, 16)

            def slots(ph, base):
                def gather(t, j, par):
                    gp.wait_ge(m_xt, SLOT_TILES * ph + t + 1)
                    gp.tensor_copy(cur[:, par, 0:1], slot_tok[:, bass.ds(t, 1)]).then_inc(s_cur, 1)
                    gp.drain()
                    gp.indirect_dma_start(xg[:, par], None, xn_rows,
                                          bass.IndirectOffsetOnAxis(ap=cur[:, par, 0:1], axis=0)).then_inc(xg_in[par], 16)

                gp.wait_ge(s_route, ph + 1)
                for par in (0, 1):
                    gp.wait_ge(g_out[par], 32 * (ph + 1) + 1)
                with gp.Fori(0, SLOT_TILES // 2) as j:
                    gather(2 * j, j, 0)
                    gather(2 * j + 1, j, 1)
                gather(SLOT_TILES - 1, SLOT_TILES // 2, 0)

            def fetch_outputs(c, i, free, base):
                n = TPC * c + i
                if free is not None:
                    gp.wait_ge(free, n - TPC + 1)
                gp.tensor_copy(cur[:, i, :], pos_i[:, :, bass.ds(n, 1)].rearrange("p a b -> p (a b)")).then_inc(s_cur, 1)
                gp.drain()
                for k in (0, 1):
                    gp.indirect_dma_start(yg[:, i, k], None, slot_out,
                                          bass.IndirectOffsetOnAxis(ap=cur[:, i, k:k + 1], axis=0)).then_inc(yg_in[i], 16)

            def add_squares(u):
                gp.wait_ge(c_sq, u + 1)
                gp.wait_ge(c_ssq, u + 1)
                gp.tensor_tensor(sqa, sqs[:, 0], sqs[:, 1], ALU.add).then_inc(c_sqa, 1)

            def add_out(c):
                for i in range(TPC):
                    n, j = TPC * c + i, 2 * c + i // 2
                    gp.wait_ge(c_ob, n + 3)
                    gp.wait_ge(x1t_in[i % 2], 16 * (j + 1))
                    gp.wait_ge(x2_st[i % 2], 16 * j + 1)
                    gp.tensor_tensor(x2t[:, i % 2], ob[:, i % 2], x1t[:, i % 2], ALU.add).then_inc(c_x2, 1)

            def outputs_stored(ph):
                for par in (0, 1):
                    gp.wait_ge(m_yst[par], 16 * (ph + 1) * (SLOT_TILES // 2 + 1 - par) + 1)

            gp.sem_inc(c_x2, 2)
            gp.sem_inc(c_sqa, 1)
            slots(0, 0)
            outputs_stored(0)
            gp.wait_ge(w_save, 16)
            for i in range(TPC):
                fetch_outputs(0, i, None, SLOT_TILES)

            def chunk(c, first, last):
                add_squares(3 * c)
                if not last:
                    for i in range(TPC):
                        fetch_outputs(c + 1, i, c_comb, SLOT_TILES)
                if not first:
                    add_out(c - 1)
                add_squares(3 * c + 1)
                add_squares(3 * c + 2)

            chunk(0, True, False)
            with gp.Fori(1, NCH - 1) as c:
                chunk(c, False, False)
            chunk(NCH - 1, False, True)
            add_out(NCH - 1)
            slots(1, SLOT_TILES + NT)
            outputs_stored(1)
            for g in range(NCH):
                for i in range(TPC):
                    fetch_outputs(g, i, f_comb if g else None, 2 * SLOT_TILES + NT)

        @block.tensor
        def _(pe):
            def transpose4(dst, src):
                for k in range(KD):
                    last = pe.transpose(dst[:, k * P:(k + 1) * P], src[:, k * P:(k + 1) * P], ident[:, :])
                return last

            def products(dst, terms):
                for n, (a, b) in enumerate(terms):
                    last = pe.matmul(dst, a, b, start=(n == 0), stop=(n == len(terms) - 1))
                return last

            def score_tiles(ph):
                o = NT * ph

                def xt(n, par, m):
                    pe.wait_ge(s_xn, o + n + 1)
                    pe.wait_ge(s_xtc, o + n + 1)
                    transpose4(bank[m % 2], lg[:, par, m % TPC]).then_inc(s_xt, 1)

                def score(n, m):
                    pe.wait_ge(s_xtc, o + n + 3)
                    products(bank[2][:, bass.ds(n * E, E)],
                             [(xnT[:, m % 2, k, :], gw[:, k, :]) for k in range(KD)]).then_inc(s_gate, 1)

                with pe.Fori(0, NCH // 2) as j:
                    for m in range(2 * TPC):
                        xt(2 * TPC * j + m, m // TPC, m)
                        if m:
                            score(2 * TPC * j + m - 1, m - 1)
                    score(2 * TPC * j + 2 * TPC - 1, 2 * TPC - 1)

            def route(ph):
                pe.wait_ge(s_onehot, ph + 1)
                chosen = M8.rearrange("p a b -> p (a b)")
                products(bank[3][:, 0:NT * E], [(before[:, :], chosen)])
                products(bank[4][:, 0:NT * E], [(ones[:, :], chosen)]).then_inc(s_count, 1)
                pe.wait_ge(s_ohs, ph + 1)
                products(bank[5][:, 0:SLOT_TILES],
                         [(OHlo[:, k, t, :], OHhi[:, k, t, 0:SLOT_TILES]) for k in (0, 1) for t in range(NT)]).then_inc(s_inv, 1)

            def slots(ph):
                o = SLOT_TILES * ph
                g = (SLOT_TILES // 2 + 1) * ph

                def xt(t, j, par):
                    pe.wait_ge(xg_in[par], 16 * (g - par * ph + j + 1))
                    pe.wait_ge(m_xl, o + t + 1)
                    transpose4(bank[par], xg[:, par]).then_inc(m_xt, 1)

                def up(t, par):
                    ev = pe.value_load(tile_exp[0:1, bass.ds(t, 1)], min_val=0, max_val=E - 1)
                    pe.wait_ge(m_xl, o + t + 3)
                    pe.wait_ge(m_zb, o + t + 1)
                    products(bank[2 + par][:, 0:HID],
                             [(a[:, par, k * P:(k + 1) * P], w1(part, k, ev))
                              for k in range(KD) for a, part in ((xh, 0), (xh, 1), (xl, 0))]).then_inc(m_z, 1)
                    return ev

                def ht(t, par):
                    pe.wait_ge(m_h, o + t + 3)
                    pe.wait_ge(m_hl, o + t + 1)
                    for c in range(KH):
                        last = pe.transpose(bank[4 + par][:, c * P:(c + 1) * P], hact[:, par, c * P:(c + 1) * P], ident[:, :])
                    last.then_inc(m_ht, 1)

                def down(t, par):
                    ev = pe.value_load(tile_exp[0:1, bass.ds(t, 1)], min_val=0, max_val=E - 1)
                    pe.wait_ge(m_hl, o + t + 3)
                    pe.wait_ge(m_yo, o + t + 1)
                    products(bank[6 + par][:, :],
                             [(a[:, par, c, :], w2(part, c, ev)) for c in range(KH)
                              for a, part in ((hh, 0), (hh, 1), (hl, 0))]).then_inc(m_y, 1)

                pe.wait_ge(s_route, ph + 1)
                if ph == 0:
                    pe.wait_ge(w_ready, E + 2)
                else:
                    pe.wait_ge(w_back, 16)
                xt(0, 0, 0)
                up(0, 0)
                xt(1, 0, 1)

                def step(t, j, par):
                    other = 1 - par
                    ht(t, par)
                    up(t + 1, other)
                    xt(t + 2, j + 1, par)
                    down(t, par)

                with pe.Fori(0, SLOT_TILES // 2 - 1) as j:
                    step(2 * j, j, 0)
                    step(2 * j + 1, j, 1)
                t = SLOT_TILES - 3
                step(t, t // 2, 0)
                ht(t + 1, 1)
                up(t + 2, 0)
                down(t + 1, 1)
                ht(t + 2, 0)
                down(t + 2, 0)

            def mixer_in(c):
                for i in range(TPC):
                    n = TPC * c + i
                    pe.wait_ge(c_xn, n + 1)
                    pe.wait_ge(c_xl, n + 1)
                    if not (isinstance(c, int) and c < 2):
                        pe.wait_ge(c_ob, TPC * (c - 1) + 2)
                    transpose4(bank[6 + i % 2], xnt[:, i % 2]).then_inc(c_xt, 1)
                pe.wait_ge(c_xl, TPC * (c + 1) + 2)
                if not (isinstance(c, int) and c == 0):
                    pe.wait_ge(c_rt, 3 * c)
                products(bank[5][0:NAB, :],
                         [(att[:, part, AB0 + k * NAB:AB0 + (k + 1) * NAB], x[:, k, :])
                          for k in range(KD) for part, x in ((0, xTh), (1, xTh), (0, xTl))]).then_inc(c_ab, 1)

            def project(c, p):
                for kind in range(KINDS):
                    m = KINDS * (PAIRS * c + p) + kind
                    col = (p * KINDS + kind) * P
                    pe.wait_ge(c_ev, m + 1)
                    products(bank[kind % 3][:, :],
                             [(att[:, part, k * NCOL + col:k * NCOL + col + P], x[:, k, :])
                              for k in range(KD) for part, x in ((0, xTh), (1, xTh), (0, xTl))]).then_inc(c_proj, 1)

            def spread(c, p):
                pe.wait_ge(c_sgl, c + 1)
                pe.wait_ge(c_scan, PAIRS * c + p + 1)
                products(bank[3][:, :], [(sel[:, 1, p, :], sigab)])
                products(bank[4][:, :], [(sel[:, 0, p, :], sigab)]).then_inc(c_bc, 1)

            def mean_square(u, c_tanh):
                pe.wait_ge(c_sqa, u + 2)
                pe.wait_ge(c_rt, u + 1)
                pe.wait_ge(c_th, c_tanh)
                products(bank[5][:, :], [(headmean[:, :], sqa)]).then_inc(c_ssq, 1)

            def project_out(c, split):
                pe.wait_ge(c_norm, PAIRS * (c + 1) + 3)
                pe.wait_ge(c_xl, split)
                for i in range(TPC):
                    pe.wait_ge(c_ob, TPC * c + i + 1)
                    products(bank[6 + i % 2][:, :],
                             [(a[:, r, i * P:(i + 1) * P], att[:, part, WO0 + r * D:WO0 + (r + 1) * D])
                              for r in range(2 * PAIRS) for a, part in ((oh, 0), (oh, 1), (ol, 0))]).then_inc(c_out, 1)

            def chunk(c, first, last):
                project(c, 0)
                spread(c, 0)
                if not first:
                    mean_square(3 * c - 1, c + 1)
                project(c, 1)
                spread(c, 1)
                mean_square(3 * c, c + 1)
                if not first:
                    project_out(c - 1, TPC * (c + 1) + 2)
                project(c, 2)
                spread(c, 2)
                mean_square(3 * c + 1, c + 1)
                if not last:
                    mixer_in(c + 1)

            for s, n in ((s_gate, 2), (m_xt, 2), (m_z, 2), (m_ht, 2), (m_y, 2), (c_xt, 2), (c_ssq, 1), (c_out, 1)):
                pe.sem_inc(s, n)
            pe.wait_ge(consts, 1)
            pe.wait_ge(params, 16 * 5)
            score_tiles(0)
            route(0)
            slots(0)
            pe.wait_ge(a_lo, PIECES + 1)
            mixer_in(0)
            chunk(0, True, False)
            with pe.Fori(1, NCH - 1) as c:
                chunk(c, False, False)
            chunk(NCH - 1, False, True)
            mean_square(3 * NCH - 1, NCH)
            project_out(NCH - 1, NT + 2)
            score_tiles(1)
            route(1)
            slots(1)

        @block.scalar
        def _(act):
            ch = Chain(act, actc)

            def normalise_groups(ph):
                o = NT * ph

                def normalise(j, par):
                    act.wait_ge(s_rstd, NCH * ph + 2 * j + par + 1)
                    for i in range(TPC):
                        act.activation(lg[:, par, i], lg[:, par, i], ACT.Identity, scale=rstd[:, par, 0, i:i + 1],
                                       bias=rstd[:, par, 1, i:i + 1]).then_inc(s_xn, 1)

                def copy_out(n, m):
                    act.wait_ge(s_xt, o + n + 1)
                    act.wait_ge(s_gate, o + n + 1)
                    act.activation(xnT[:, m % 2].rearrange("p k c -> p (k c)"), bank[m % 2][:, :], ACT.Copy).then_inc(s_xtc, 1)

                with act.Fori(0, NCH // 2) as j:
                    for par in (0, 1):
                        normalise(j, par)
                        for i in range(TPC):
                            copy_out(2 * TPC * j + TPC * par + i, TPC * par + i)

            def slots(ph):
                o = SLOT_TILES * ph

                def x_high(t, par):
                    act.wait_ge(m_xt, o + t + 3)
                    act.wait_ge(m_z, o + t + 1)
                    act.activation(xh[:, par], bank[par][:, :], ACT.Copy).then_inc(m_xh, 1)

                def silu(t, par):
                    act.wait_ge(m_zb, o + t + 3)
                    act.wait_ge(m_ht, o + t + 1)
                    act.activation(hact[:, par, 0:HID], z[:, par], ACT.Silu).then_inc(m_h, 1)

                def h_high(t, par):
                    act.wait_ge(m_ht, o + t + 3)
                    act.wait_ge(m_y, o + t + 1)
                    act.activation(hh[:, par].rearrange("p a b -> p (a b)"), bank[4 + par][:, 0:KH * P], ACT.Copy).then_inc(m_hh, 1)

                def piece(q):
                    act.wait_ge(a_in, 16 * (q + 1))
                    act.activation(att[:, 0, bass.ds(q * PIECE, PIECE)], apiece, ACT.Copy, scale=WSCALE).then_inc(a_hi, 1)

                def step(t, par):
                    h_high(t, par)
                    silu(t + 1, 1 - par)
                    x_high(t + 2, par)

                if ph == 0:
                    act.wait_ge(w_ready, E + 2)
                x_high(0, 0)
                silu(0, 0)
                x_high(1, 1)
                split = 0 if ph else PIECES
                if split:
                    with act.Fori(0, split) as j:
                        step(2 * j, 0)
                        step(2 * j + 1, 1)
                        piece(j)
                with act.Fori(split, SLOT_TILES // 2 - 1) as j:
                    step(2 * j, 0)
                    step(2 * j + 1, 1)
                t = SLOT_TILES - 3
                step(t, 0)
                h_high(t + 1, 1)
                silu(t + 2, 0)
                h_high(t + 2, 0)

            def normalise(c, i):
                act.wait_ge(c_rstd, c + 1)
                act.wait_ge(c_xt, TPC * c + i + 1)
                act.activation(xnt[:, i % 2], xgrp[:, i], ACT.Identity, scale=rstd[:, 0, 0, i:i + 1],
                               bias=rstd[:, 0, 1, i:i + 1]).then_inc(c_xn, 1)

            def x_high(c, i):
                act.wait_ge(c_xt, TPC * c + i + 3)
                act.activation(xTh[:, :, i * P:(i + 1) * P], bank[6 + i % 2][:, :].rearrange("p (k c) -> p k c", k=KD),
                               ACT.Copy).then_inc(c_xh, 1)

            def chunk_in(c):
                for i in range(TPC):
                    x_high(c, i)
                    if i + 2 < TPC:
                        normalise(c, i + 2)
                act.wait_ge(c_ab, c + 1)
                act.activation(abt[0:NAB], bank[5][0:NAB, :], ACT.Tanh, scale=0.5 * UNSCALE).then_inc(c_th, 1)
                act.wait_ge(c_sig, c + 1)
                if not (isinstance(c, int) and c == 0):
                    act.wait_ge(c_bc, PAIRS * c)
                act.activation(sigab[0:NAB], abs_[0:NAB], ACT.Copy).then_inc(c_sgh, 1)

            def evacuate(c, p, kinds):
                u = PAIRS * c + p
                for kind in kinds:
                    act.wait_ge(c_proj, KINDS * u + kind + 1)
                    if kind < 4:
                        act.wait_ge(c_conv, u + 1)
                        act.activation(raw[:, p, kind, HALO:], bank[kind % 3][:, :], ACT.Copy, scale=UNSCALE).then_inc(c_ev, 1)
                    else:
                        act.wait_ge(c_norm, u + 1)
                        act.activation(sg[:, p, kind - 4], bank[kind % 3][:, :], ACT.Silu, scale=UNSCALE).then_inc(c_ev, 1)

            def trig(u):
                act.wait_ge(c_frac, u + 1)
                act.activation(sn, frac, ACT.Sin, scale=PI2)
                ch(act.activation(af, frac, ACT.Abs))
                ch.wait()
                act.activation(cs, af, ACT.Sin, scale=-PI2, bias=half_pi[:, 0:1]).then_inc(c_trig, 1)

            def root(u):
                act.wait_ge(c_ssq, u + 2)
                act.wait_ge(c_norm, u + 3)
                act.activation(rt, bank[5][:, :], ACT.Sqrt, bias=epsc[:, 0:1]).then_inc(c_rt, 1)

            def squares(u):
                act.wait_ge(c_scan, u + 2)
                act.wait_ge(c_sqa, u + 1)
                for eo in (0, 1):
                    last = act.activation(sqs[:, eo], res[:, u_pair[0], eo], ACT.Square)
                last.then_inc(c_sq, 1)

            u_pair = [0]

            def chunk(n, c, first, last):
                allk = range(KINDS)
                evacuate(c, 1, (0, 1))
                trig(3 * c)
                if not first:
                    root(3 * c - 1)
                evacuate(c, 1, (2, 3, 4, 5))
                u_pair[0] = 0
                squares(3 * c)
                trig(3 * c + 1)
                root(3 * c)
                if not first:
                    out_tiles(c - 1)
                evacuate(c, 2, allk)
                u_pair[0] = 1
                squares(3 * c + 1)
                if not last:
                    normalise(c + 1, 0)
                    normalise(c + 1, 1)
                trig(3 * c + 2)
                root(3 * c + 1)
                if not last:
                    chunk_in(c + 1)
                    evacuate(c + 1, 0, allk)
                u_pair[0] = 2
                squares(3 * c + 2)

            def out_tiles(c):
                for i in range(TPC):
                    n = TPC * c + i
                    act.wait_ge(c_out, n + 2)
                    act.wait_ge(c_x2, n + 1)
                    act.activation(ob[:, i % 2], bank[6 + i % 2][:, :], ACT.Copy, scale=UNSCALE).then_inc(c_ob, 1)

            for s, n in ((s_xtc, 2), (m_h, 2), (c_ev, 3), (c_rt, 1), (c_ob, 2)):
                act.sem_inc(s, n)
            act.wait_ge(consts, 1)
            normalise_groups(0)
            act.wait_ge(s_dm, 1)
            act.activation(th, dm, ACT.Tanh, scale=0.5).then_inc(s_tanh, 1)
            with act.Fori(0, E // 2) as j:
                for par in (0, 1):
                    act.wait_ge(w_in[par], 16 * (j + 1))
                    act.activation(wexp[:, bass.ds(2 * j + par, 1), 0:FW].rearrange("p a w -> p (a w)"), wstage[:, par],
                                   ACT.Copy, scale=WSCALE).then_inc(w_hi, 1)
            slots(0)
            normalise(0, 0)
            normalise(0, 1)
            chunk_in(0)
            evacuate(0, 0, range(KINDS))
            chunk(0, 0, True, False)
            ch.loop(1, NCH - 1, 3, lambda c: chunk(None, c, False, False))
            chunk(None, NCH - 1, False, True)
            root(3 * NCH - 1)
            out_tiles(NCH - 1)
            normalise_groups(1)
            act.wait_ge(s_dm, 2)
            act.activation(th, dm, ACT.Tanh, scale=0.5).then_inc(s_tanh, 1)
            slots(1)

        @block.vector
        def _(v):
            ch = Chain(v, dve)

            def seq(ins):
                ch(ins)
                ch.wait()

            def inv_std(par, done):
                a, y, t1 = nt4[:, 0], nt4[:, 1], nt4[:, 2]
                ch(v.tensor_tensor(mv[:, :, 0], bst[:, :, 1], bst[:, :, 4], ALU.add))
                ch(v.tensor_tensor(mv[:, :, 1], bst[:, :, 1], bst[:, :, 4], ALU.subtract))
                seq(v.tensor_tensor(a, bst[:, :, 2], bst[:, :, 5], ALU.add))
                ch(v.scalar_tensor_tensor(t1, mv[:, :, 1], 0.25, mv[:, :, 1], ALU.mult, ALU.mult))
                seq(v.tensor_scalar(a, a, 1.0 / D, EPS, ALU.mult, ALU.add))
                seq(v.tensor_tensor(a, a, t1, ALU.add))
                seq(v.tensor_scalar(y.bitcast(I32), a.bitcast(I32), -0.5, RSQRT_SEED, ALU.mult, ALU.add))
                for _ in range(3):
                    seq(v.tensor_tensor(t1, y, y, ALU.mult))
                    seq(v.scalar_tensor_tensor(t1, t1, -0.5, a, ALU.mult, ALU.mult))
                    seq(v.scalar_tensor_tensor(y, t1, 1.5, y, ALU.add, ALU.mult))
                v.tensor_copy(rstd[:, par, 0], y)
                v.scalar_tensor_tensor(rstd[:, par, 1], mv[:, :, 0], -0.5, y, ALU.mult, ALU.mult).then_inc(done, 1)

            def stats(rows):
                for i in range(TPC):
                    ch(v.bn_stats(bst[:, i], rows[:, i]))
                ch.wait()

            def group_stats(ph):
                def turn(j):
                    for par in (0, 1):
                        v.wait_ge(g_in[par], 16 * (2 * ph + j + 1))
                        stats(lg[:, par])
                        inv_std(par, s_rstd)
                ch.loop(0, NCH // 2, 2 * (TPC + 16), turn)

            def round_down(dst, src, tmp_):
                seq(v.tensor_scalar(tmp_, src, -63.5, 1.0 / P, ALU.add, ALU.mult))
                seq(v.tensor_scalar(dst, tmp_, MAGIC, MAGIC, ALU.add, ALU.subtract))

            def route(ph):
                def bc(x):
                    return x.unsqueeze(2).to_broadcast([P, NT, E])

                def eb(x):
                    return x.unsqueeze(2).to_broadcast([P, E, NT])

                flat = "p a b -> p (a b)"
                v.wait_ge(s_gate, NT * (ph + 1) + 2)
                if ph == 0:
                    seq(v.tensor_tensor(gb[:, 0], gb[:, 0], gb[:, 1], ALU.add))
                seq(v.tensor_tensor(S, bank[2][:, 0:NT * E].rearrange("p (a b) -> p a b", b=E),
                                    gb[:, 0].unsqueeze(1).to_broadcast([P, NT, E]), ALU.add))
                seq(v.reduce_max(m1, S, AX))
                seq(v.tensor_tensor(KEY, S, bc(m1), ALU.is_equal))
                seq(v.tensor_tensor(KEY, KEY, desc[:, :, :], ALU.mult))
                seq(v.reduce_max(k1, KEY, AX))
                seq(v.tensor_tensor(OH1, desc[:, :, :], bc(k1), ALU.is_equal))
                seq(v.scalar_tensor_tensor(S2.rearrange(flat), OH1.rearrange(flat), 0.0, S.rearrange(flat), ALU.is_equal, ALU.mult))
                seq(v.scalar_tensor_tensor(S2.rearrange(flat), OH1.rearrange(flat), -3.0e38, S2.rearrange(flat), ALU.mult, ALU.add))
                seq(v.reduce_max(k1, S2, AX))
                v.tensor_tensor(dm, k1, m1, ALU.subtract).then_inc(s_dm, 1)
                seq(v.tensor_tensor(KEY, S2, bc(k1), ALU.is_equal))
                seq(v.tensor_tensor(KEY, KEY, desc[:, :, :], ALU.mult))
                seq(v.reduce_max(k1, KEY, AX))
                seq(v.tensor_tensor(OH2, desc[:, :, :], bc(k1), ALU.is_equal))
                v.tensor_tensor(M8, OH1, OH2, ALU.add).then_inc(s_onehot, 1)
                v.wait_ge(s_tanh, ph + 1)
                v.tensor_scalar(ghalf[:, 0], th, -0.25, 0.25, ALU.mult, ALU.add)
                v.tensor_scalar(ghalf[:, 1], th, 0.25, 0.25, ALU.mult, ALU.add)
                seq(v.memset(one8, 1.0))
                v.wait_ge(s_count, ph + 1)
                seq(v.tensor_copy(CE, bank[4][:, 0:NT * E].rearrange("p (t e) -> p e t", e=E)))
                seq(v.tensor_tensor_scan(SC.rearrange(flat), restart[:, :, :].rearrange(flat), CE.rearrange(flat), 0.0, ALU.mult, ALU.add))
                ch(v.tensor_tensor(EX, SC, CE, ALU.subtract))
                seq(v.tensor_scalar(tl, SC[:, :, NT - 1], float(P - 1), None, ALU.add))
                round_down(tl, tl, st8)
                seq(v.tensor_tensor_scan(en, one8, tl, 0.0, ALU.mult, ALU.add))
                seq(v.tensor_tensor(st8, en, tl, ALU.subtract))
                seq(v.tensor_scalar(base8, st8, float(P), None, ALU.mult))
                seq(v.tensor_tensor(EX, EX, eb(base8), ALU.add))
                seq(v.tensor_tensor(QP, bank[3][:, 0:NT * E].rearrange("p (a b) -> p a b", b=E),
                                    EX.rearrange("p e t -> p t e"), ALU.add))
                for k, oh_ in ((0, OH1), (1, OH2)):
                    seq(v.tensor_tensor(KEY, QP, oh_, ALU.mult))
                    seq(v.reduce_sum(posf[:, k], KEY, AX))
                ch(v.tensor_copy(pos_i[:, :, :], posf))
                round_down(hi_f, posf, lo_f)
                seq(v.scalar_tensor_tensor(lo_f, hi_f, -float(P), posf, ALU.mult, ALU.add))
                for k in (0, 1):
                    ch(v.tensor_tensor(OHlo[:, k], lo_f[:, k].unsqueeze(2).to_broadcast([P, NT, P]),
                                       lane[:, :].unsqueeze(1).to_broadcast([P, NT, P]), ALU.is_equal))
                    seq(v.tensor_tensor(OHhi[:, k, :, 0:SLOT_TILES], hi_f[:, k].unsqueeze(2).to_broadcast([P, NT, SLOT_TILES]),
                                        lane[:, 0:SLOT_TILES].unsqueeze(1).to_broadcast([P, NT, SLOT_TILES]), ALU.is_equal))
                    last = v.tensor_tensor(OHhi[:, k, :, 0:SLOT_TILES], OHhi[:, k, :, 0:SLOT_TILES],
                                           tokid[:, :].unsqueeze(2).to_broadcast([P, NT, SLOT_TILES]), ALU.mult)
                    if k == 0:
                        ch(last)
                last.then_inc(s_ohs, 1)
                seq(v.tensor_tensor(cmp, lane[:, 0:SLOT_TILES].unsqueeze(2).to_broadcast([P, SLOT_TILES, E]),
                                    en.unsqueeze(1).to_broadcast([P, SLOT_TILES, E]), ALU.is_ge))
                seq(v.reduce_sum(evf, cmp, AX))
                seq(v.tensor_scalar(tile_exp[:, :], evf, float(E - 1), None, ALU.min))
                v.wait_ge(s_inv, ph + 1)
                v.tensor_copy(slot_tok[:, :], bank[5][:, 0:SLOT_TILES]).then_inc(s_route, 1)

            def slots(ph):
                o = SLOT_TILES * ph

                def x_low(t, par):
                    v.wait_ge(m_xh, o + t + 1)
                    v.tensor_tensor(xl[:, par], bank[par][:, :], xh[:, par], ALU.subtract).then_inc(m_xl, 1)

                def add_bias(t, par):
                    ev = v.value_load(tile_exp[0:1, bass.ds(t, 1)], min_val=0, max_val=E - 1)
                    v.wait_ge(m_z, o + t + 3)
                    v.wait_ge(m_h, o + t + 1)
                    v.scalar_tensor_tensor(z[:, par], bank[2 + par][:, 0:HID], UNSCALE, b1_bc[:, bass.ds(ev * HID, HID)],
                                           ALU.mult, ALU.add).then_inc(m_zb, 1)

                def h_low(t, par):
                    v.wait_ge(m_hh, o + t + 1)
                    v.tensor_tensor(hl[:, par].rearrange("p a b -> p (a b)"), bank[4 + par][:, 0:KH * P],
                                    hh[:, par].rearrange("p a b -> p (a b)"), ALU.subtract).then_inc(m_hl, 1)

                def y_out(t, j, par):
                    v.wait_ge(m_y, o + t + 3)
                    v.wait_ge(m_yst[par], 16 * ((SLOT_TILES // 2 + 1 - par) * ph + j) + 1)
                    v.tensor_scalar(yo[:, par], bank[6 + par][:, :], UNSCALE, None, ALU.mult).then_inc(m_yo, 1)

                def piece(q):
                    v.wait_ge(a_hi, q + 1)
                    v.scalar_tensor_tensor(att[:, 1, bass.ds(q * PIECE, PIECE)], apiece, WSCALE,
                                           att[:, 0, bass.ds(q * PIECE, PIECE)], ALU.mult, ALU.subtract).then_inc(a_lo, 1)

                def step(t, j, par):
                    h_low(t, par)
                    add_bias(t + 1, 1 - par)
                    x_low(t + 2, par)
                    y_out(t, j, par)

                for par in (0, 1):
                    v.wait_ge(g_out[par], 32 * (ph + 1) + 1)
                v.memset(hact[:, :, HID:HID + 1], 1.0)
                seq(v.memset(hact[:, :, HID + 1:KH * P], 0.0))
                v.wait_ge(b1_in[ph], 16)
                x_low(0, 0)
                add_bias(0, 0)
                x_low(1, 1)
                split = 0 if ph else PIECES
                if split:
                    with v.Fori(0, split) as j:
                        step(2 * j, j, 0)
                        step(2 * j + 1, j, 1)
                        piece(j)
                with v.Fori(split, SLOT_TILES // 2 - 1) as j:
                    step(2 * j, j, 0)
                    step(2 * j + 1, j, 1)
                t = SLOT_TILES - 3
                step(t, t // 2, 0)
                h_low(t + 1, 1)
                add_bias(t + 2, 0)
                y_out(t + 1, t // 2, 1)
                h_low(t + 2, 0)
                y_out(t + 2, t // 2 + 1, 0)

            def combine(g, arrived, uses, done):
                v.wait_ge(arrived, 16 * (g + 1))
                for i in range(TPC):
                    n = TPC * g + i
                    v.wait_ge(yg_in[i], 32 * (uses + g + 1))
                    seq(v.scalar_tensor_tensor(xgrp[:, i], yg[:, i, 0], ghalf[:, 0, bass.ds(n, 1)], xgrp[:, i], ALU.mult, ALU.add))
                    v.scalar_tensor_tensor(xgrp[:, i], yg[:, i, 1], ghalf[:, 1, bass.ds(n, 1)], xgrp[:, i], ALU.mult, ALU.add).then_inc(done, 1)

            def chunk_stats(c):
                combine(c, cg_in, 0, c_comb)
                v.wait_ge(c_comb, TPC * (c + 1))
                stats(xgrp)
                inv_std(0, c_rstd)

            def chunk_low(c):
                for i in range(TPC):
                    v.wait_ge(c_xh, TPC * c + i + 1)
                    v.tensor_tensor(xTl[:, :, i * P:(i + 1) * P], bank[6 + i % 2][:, :].rearrange("p (k c) -> p k c", k=KD),
                                    xTh[:, :, i * P:(i + 1) * P], ALU.subtract).then_inc(c_xl, 1)
                v.wait_ge(c_th, c + 1)
                v.tensor_scalar(abs_[0:NAB], abt[0:NAB], 0.5, 0.5, ALU.mult, ALU.add).then_inc(c_sig, 1)
                v.wait_ge(c_sgh, c + 1)
                v.tensor_tensor(sigab[32:32 + NAB], abs_[0:NAB], sigab[0:NAB], ALU.subtract).then_inc(c_sgl, 1)

            def angles(c, p):
                u = PAIRS * c + p
                v.wait_ge(c_ev, KINDS * u + 2 + 3)
                seq(v.tensor_scalar(ang, raw[:, p, 0, 0:CH], cang[:, p, 0, 0:1], None, ALU.mult))
                for kind, j in [(0, 1), (0, 2), (0, 3), (1, 0), (1, 1), (1, 2), (1, 3)]:
                    seq(v.scalar_tensor_tensor(ang, raw[:, p, kind, j:j + CH], cang[:, p, kind, j:j + 1], ang, ALU.mult, ALU.add))
                seq(v.tensor_scalar(rnd, ang, MAGIC, MAGIC, ALU.add, ALU.subtract))
                v.tensor_tensor(frac, ang, rnd, ALU.subtract).then_inc(c_frac, 1)
                v.wait_ge(c_ev, KINDS * u + 4 + 3)
                for eo in (0, 1):
                    ch(v.tensor_scalar(vcon[:, eo], raw[:, p, 2 + eo, 0:CH], conv_sb[:, p, 2 + eo, 0:1], None, ALU.mult))
                for j in range(1, TAPS):
                    for eo in (0, 1):
                        ch.wait(ch.n - 1)
                        ch(v.scalar_tensor_tensor(vcon[:, eo], raw[:, p, 2 + eo, j:j + CH], conv_sb[:, p, 2 + eo, j:j + 1],
                                                  vcon[:, eo], ALU.mult, ALU.add))
                ch.wait()
                v.tensor_copy(raw[:, p, :, 0:HALO], raw[:, p, :, CH:CH + HALO]).then_inc(c_conv, 1)

            def recur(c, p):
                u = PAIRS * c + p
                v.wait_ge(c_trig, u + 1)
                v.wait_ge(c_bc, u + 1)
                ch(v.tensor_tensor(sn, bank[3][:, :], sn, ALU.mult))
                ch(v.tensor_tensor(cs, bank[3][:, :], cs, ALU.mult))
                ch.wait()
                ch(v.tensor_tensor(tmp[:, 0], vcon[:, 0], cs, ALU.mult))
                ch(v.tensor_tensor(tmp[:, 1], vcon[:, 1], sn, ALU.mult))
                ch(v.tensor_tensor(tmp[:, 2], vcon[:, 1], cs, ALU.mult))
                ch(v.tensor_tensor(tmp[:, 3], vcon[:, 0], sn, ALU.mult))
                ch.wait(ch.n - 2)
                ch(v.tensor_tensor(tmp[:, 0], tmp[:, 0], tmp[:, 1], ALU.subtract))
                ch.wait(ch.n - 1)
                ch(v.tensor_tensor(tmp[:, 2], tmp[:, 2], tmp[:, 3], ALU.add))
                ch.wait(ch.n - 1)
                v.tensor_tensor_scan(res[:, p, 0], bank[4][:, :], tmp[:, 0], carry[:, p, 0:1], ALU.mult, ALU.add)
                ch.wait()
                v.tensor_tensor_scan(res[:, p, 1], bank[4][:, :], tmp[:, 2], carry[:, p, 1:2], ALU.mult, ALU.add).then_inc(c_scan, 1)
                v.wait_ge(c_scan, u + 2)
                seq(v.tensor_copy(carry[:, p, :], res[:, p, :, CH - 1]))

            def gate(c, p):
                u = PAIRS * c + p
                v.wait_ge(c_rt, u + 2)
                v.wait_ge(c_ev, KINDS * (u + 1) + 3)
                v.wait_ge(c_out, TPC * c + 1)
                seq(v.reciprocal(ri, rt))
                for eo in (0, 1):
                    ch(v.scalar_tensor_tensor(on[:, eo], res[:, p, eo], rms_sb[:, eo:eo + 1], ri, ALU.mult, ALU.mult))
                for eo in (0, 1):
                    ch.wait(ch.n - 1)
                    ch(v.tensor_tensor(on[:, eo], on[:, eo], sg[:, p, eo], ALU.mult))
                for eo in (0, 1):
                    ch.wait(ch.n - 1)
                    ch(v.tensor_copy(oh[:, 2 * p + eo], on[:, eo]))
                ch.wait(ch.n - 1)
                v.tensor_tensor(ol[:, 2 * p], on[:, 0], oh[:, 2 * p], ALU.subtract)
                ch.wait()
                v.tensor_tensor(ol[:, 2 * p + 1], on[:, 1], oh[:, 2 * p + 1], ALU.subtract).then_inc(c_norm, 1)

            def chunk(c, first, last):
                angles(c, 0)
                recur(c, 0)
                if not first:
                    gate(c - 1, 2)
                angles(c, 1)
                recur(c, 1)
                gate(c, 0)
                if not last:
                    chunk_stats(c + 1)
                angles(c, 2)
                if not last:
                    chunk_low(c + 1)
                recur(c, 2)
                gate(c, 1)

            for s, n in ((m_xl, 2), (m_zb, 2), (m_hl, 2), (m_yo, 2), (w_ready, 2), (a_lo, 1), (c_xl, 2),
                         (c_conv, 3), (c_norm, 3), (c_scan, 1)):
                v.sem_inc(s, n)
            group_stats(0)
            v.wait_ge(consts, 1)
            v.wait_ge(params, 16 * 5)
            route(0)
            for p in range(PAIRS):
                for kind in (0, 1):
                    ch(v.tensor_scalar(cang[:, p, kind], conv_sb[:, p, kind], turns_sb[:, kind:kind + 1], None, ALU.mult))
            with v.Fori(0, E // 2) as j:
                for par in (0, 1):
                    e = 2 * j + par
                    v.wait_ge(w_hi, e + 1)
                    v.scalar_tensor_tensor(wexp[:, bass.ds(e, 1), FW:2 * FW].rearrange("p a w -> p (a w)"), wstage[:, par],
                                           WSCALE, wexp[:, bass.ds(e, 1), 0:FW].rearrange("p a w -> p (a w)"),
                                           ALU.mult, ALU.subtract).then_inc(w_ready, 1)
            slots(0)
            for par in (0, 1):
                v.wait_ge(m_yst[par], 16 * (SLOT_TILES // 2 + 1 - par) + 1)
            v.wait_ge(w_save, 16)
            v.memset(raw[:, :, :, 0:HALO], 0.0)
            v.memset(carry, 0.0)
            seq(v.memset(sigab, 0.0))
            chunk_stats(0)
            chunk_low(0)
            chunk(0, True, False)
            ch.loop(1, NCH - 1, CHUNK_STEPS, lambda c: chunk(c, False, False))
            chunk(NCH - 1, False, True)
            gate(NCH - 1, 2)
            group_stats(1)
            route(1)
            slots(1)
            for g in range(NCH):
                combine(g, f_in, NCH, f_comb)


def kernel(**inputs):
    import concourse.bacc as bacc
    from concourse.bass_utils import run_bass_kernel_spmd as run

    def given(name):
        return np.asarray(inputs["L0_" + name])

    w1 = given("ffn_w1").transpose(2, 0, 1).reshape(KD, P, E, HID).transpose(2, 1, 0, 3).reshape(E, P, KD * HID)
    w2 = np.zeros((E, KH * P, D), np.float32)
    w2[:, 0:HID] = given("ffn_w2").transpose(0, 2, 1)
    w2[:, HID] = given("ffn_b2")
    w2 = w2.reshape(E, KH, P, D).transpose(0, 2, 1, 3).reshape(E, P, KH * D)

    def pairs(w, eo):
        return w[:, eo::2].reshape(w.shape[0], PAIRS, 1, P)

    wq, wk, wv, wg = (given("attn_" + n) for n in ("Wq", "Wk", "Wv", "Wg"))
    cols = np.concatenate([pairs(wq, 0), pairs(wk, 0), pairs(wv, 0), pairs(wv, 1), pairs(wg, 0), pairs(wg, 1)], 2)
    ab = np.concatenate([given("attn_Wa"), given("attn_Wb")], 1)
    wo = given("attn_Wo").reshape(PAIRS, P, 2, D).transpose(1, 0, 2, 3)
    att_w = np.concatenate([cols.reshape(KD, P, NCOL).transpose(1, 0, 2).reshape(P, -1),
                            ab.reshape(KD, P, NAB).transpose(1, 0, 2).reshape(P, -1), wo.reshape(P, -1)], 1)
    cq, ck, cv = (given("attn_conv_" + n).reshape(PAIRS, P, 2, TAPS) for n in "qkv")
    conv = np.stack([cq[:, :, 0], ck[:, :, 0], cv[:, :, 0], cv[:, :, 1]], 2).transpose(1, 0, 2, 3)
    rms = given("attn_rms_w").reshape(64, 2)
    freq = 1.0 / 10000.0 ** (np.arange(0, P, 2, dtype=np.float32) / P)
    turn = np.tile(freq / (2 * np.pi), 2)
    arrays = {
        "x_in": given("attn_hidden_states").reshape(T, D),
        "ffn_w": np.concatenate([w1, w2], 2),
        "gate_wT": given("ffn_gate_w").T,
        "gate_bias": np.stack([given("ffn_gate_b"), given("ffn_bias")]),
        "b1": given("ffn_b1").reshape(E * HID),
        "att_w": att_w,
        "conv": conv,
        "rms_w": np.concatenate([rms, rms]),
        "turns": np.stack([-turn, turn], 1).astype(np.float32),
    }
    arrays = {k: np.ascontiguousarray(a) for k, a in arrays.items()}
    nc = bacc.Bacc("TRN2", target_bir_lowering=False, num_devices=1)
    args = [nc.dram_tensor(k, a.shape, mybir.dt.from_np(a.dtype), kind="ExternalInput").ap() for k, a in arrays.items()]
    out = nc.dram_tensor("out", (T, D), F32, kind="ExternalOutput").ap()
    build(nc, *args, out)
    r = run(nc, [arrays], core_ids=[0])
    return r.results[0]["out"].reshape(1, T, D)
```

```python
from contextlib import ExitStack

import numpy as np

import concourse.bass as bass
from concourse import mybir

F32, F16, I32 = mybir.dt.float32, mybir.dt.float16, mybir.dt.int32
ACT = mybir.ActivationFunctionType
ALU = mybir.AluOpType
AX = mybir.AxisListType.X

P = 128
T, D = 2048, 512
E, HID = 8, 352
NT = T // P
KD = D // P
KH = 3
LAST = HID - 2 * P
SLOT_TILES = (2 * T + E * (P - 1)) // P
FW = KD * HID + KH * D
HEADS = 6
PAIRS = HEADS // 2
KINDS = 6
TAPS = 4
CH = 512
NCH = T // CH
TPC = CH // P
HALO = TAPS - 1
NCOL = PAIRS * KINDS * P
NAB = 2 * HEADS
AW = KD * NCOL + KD * NAB + 2 * PAIRS * D
AB0, WO0 = KD * NCOL, KD * NCOL + KD * NAB
PIECES = 12
STAGES = 4
PIECE = AW // PIECES
WSCALE = 256.0
UNSCALE = 1.0 / WSCALE
EPS = 1e-5
MAGIC = 12582912.0
RSQRT_SEED = float(0x5F3759DF)
PI2 = float(2 * np.pi)
CHUNK_STEPS = 120


class Chain:

    def __init__(self, eng, sem):
        self.eng, self.sem, self.base, self.n = eng, sem, 0, 0

    def __call__(self, ins):
        self.n += 1
        ins.then_inc(self.sem, 1)
        return self.n

    def wait(self, token=None):
        self.eng.wait_ge(self.sem, self.base + (self.n if token is None else token))

    def loop(self, lo, hi, per, body):
        start, self.n = self.base + self.n, 0
        with self.eng.Fori(lo, hi) as i:
            self.base = start + (i - lo) * per
            body(i)
            assert self.n == per, (self.n, per)
        self.base, self.n = start + (hi - lo) * per, 0


def build(nc, x_in, ffn_w, gate_wT, gate_bias, b1, att_w, conv, rms_w, turns, out):
    ctx = ExitStack()
    with ctx:
        def sb(name, shape, dt=F32):
            return ctx.enter_context(nc.sbuf_tensor(name, shape, dt))

        def sem(name):
            return ctx.enter_context(nc.semaphore(name))

        def dram(name, shape, dt=F32):
            return nc.dram_tensor(name, shape, dt).ap()

        xn_rows = dram("xn_rows", (T, D))
        slot_out = dram("slot_out", (SLOT_TILES * P, D))
        x1_rows = dram("x1_rows", (T, D))
        x2_rows = dram("x2_rows", (T, D))
        w_saved = dram("w_saved", (E, P, 2 * FW), F16)

        att = sb("att", [P, 2, AW], F16)
        ident = sb("ident", [P, P])
        ones = sb("ones", [P, P])
        before = sb("before", [P, P])
        headmean = sb("headmean", [P, P])
        sel = sb("sel", [44, 2, PAIRS, P], F16)
        desc = sb("desc", [P, NT, E])
        lane = sb("lane", [P, P])
        tokid = sb("tokid", [P, NT])
        power = sb("power", [P, TPC, 2])
        restart = sb("restart", [P, E, NT])
        half_pi = sb("half_pi", [P, 1])
        epsc = sb("epsc", [P, 1])
        conv_sb = sb("conv_sb", [P, PAIRS, 4, TAPS])
        cang = sb("cang", [P, PAIRS, 2, TAPS])
        rms_sb = sb("rms_sb", [P, 2])
        turns_sb = sb("turns_sb", [P, 2])
        gw = sb("gw", [P, KD, E])
        gb = sb("gb", [P, 2, E])
        pos_i = sb("pos_i", [P, 2, NT], I32)
        ghalf = sb("ghalf", [P, 2, NT])
        slot_tok = sb("slot_tok", [P, SLOT_TILES], I32)
        tile_exp = sb("tile_exp", [P, SLOT_TILES], I32)
        mv = sb("mv", [P, TPC, 2])
        bst = sb("bst", [P, TPC, 6])
        nt4 = sb("nt4", [P, 4, TPC])
        rstd = sb("rstd", [P, NCH, 2, TPC])

        ARENA = 38800
        arena = sb("arena", [P, ARENA])

        class Layout:
            def __init__(self, at=0):
                self.at = at

            def __call__(self, shape, dt=F32, rows=P):
                n = int(np.prod(shape))
                words = n if dt != F16 else (n + 1) // 2
                v = arena[0:rows, self.at:self.at + words]
                self.at += words
                assert self.at <= ARENA, self.at
                if dt != F32:
                    v = v.bitcast(dt)
                if len(shape) > 1:
                    names = " ".join("abcd"[:len(shape)])
                    v = v.rearrange(f"p ({names}) -> p {names}", **dict(zip("abcd", shape)))
                return v

        lay = Layout()
        wexp = lay([E, 2 * FW], F16)
        wflat = arena[:, 0:E * FW].bitcast(F16)
        b1_bc = lay([E * HID])
        moe_at = lay.at
        xg = lay([2, D])
        xh, xl = lay([2, D], F16), lay([2, D], F16)
        z = lay([2, HID])
        hact = lay([2, KH * P])
        hh, hl = lay([2, KH, P], F16), lay([2, KH, P], F16)
        yo = lay([2, D])
        lay2 = Layout(moe_at)
        lg = lay2([NCH, TPC, D])
        xnT = lay2([2, KD, P])
        late = Layout(lay.at)
        OHlo = late([2, NT, P], F16)
        OHhi = late([2, NT, SLOT_TILES + 1], F16)
        apiece = Layout(lay.at)([PIECE])
        lay = Layout(max(late.at, lay2.at))
        S, S2, OH1, OH2, KEY, M8, QP = (lay([NT, E]) for _ in range(7))
        CE, SC, EX = (lay([E, NT]) for _ in range(3))
        m1, m2, k1, dm, th = (lay([NT]) for _ in range(5))
        posf, hi_f, lo_f = (lay([2, NT]) for _ in range(3))
        tl, en, st8, base8, one8 = (lay([E]) for _ in range(5))
        cmp = lay([SLOT_TILES, E])
        evf = lay([SLOT_TILES])
        wstage = att[:, :, :].rearrange("p a b -> p (a b)")[:, 0:STAGES * 2 * FW].bitcast(F32)\
            .rearrange("p (s w) -> p s w", s=STAGES)

        lay = Layout()
        raw = lay([PAIRS, 4, CH + HALO])
        xgrp = lay([TPC, D])
        yg = lay([TPC, 2, D])
        xnt = lay([2, D])
        xTh, xTl = lay([KD, CH], F16), lay([KD, CH], F16)
        abt, abs_ = lay([CH], rows=44), lay([CH], rows=44)
        sigab = lay([CH], F16, rows=44)
        sg = lay([PAIRS, 2, CH])
        ang, rnd, frac, sn, af, cs = (lay([CH]) for _ in range(6))
        vcon = lay([2, CH])
        tmp = lay([4, CH])
        res = lay([PAIRS, 2, CH])
        carry = lay([PAIRS, 2])
        sqs = lay([2, CH])
        sqa = lay([CH])
        msq, root_ = lay([TPC, 2]), lay([TPC, 2])
        rootb = lay([TPC, 2, P // 2])
        on = lay([2, CH])
        oh, ol = lay([2 * PAIRS, CH], F16), lay([2 * PAIRS, CH], F16)
        ob = lay([2, D])
        x1t = lay([2, D])
        x2t = lay([2, D])

        bank = [ctx.enter_context(nc.psum_tensor(f"bank{i}", [P, 512], F32)) for i in range(8)]

        def w1(part, k, ev):
            return wflat[:, bass.ds(ev * (2 * FW) + (part * FW + k * HID), HID)]

        def w2(part, c, ev):
            return wflat[:, bass.ds(ev * (2 * FW) + (part * FW + KD * HID + c * D), D)]

        consts = sem("consts")
        params = sem("params")
        b1_in = [sem("b1_in"), sem("b1_back")]
        w_in = [sem(f"w_in{i}") for i in range(STAGES)]
        w_hi = sem("w_hi")
        w_ready = sem("w_ready")
        w_save = sem("w_save")
        w_back = sem("w_back")
        a_in = sem("a_in")
        a_hi, a_lo = sem("a_hi"), sem("a_lo")
        g_in = [sem(f"g_in{i}") for i in range(NCH)]
        s_rstd = sem("s_rstd")
        s_xn = sem("s_xn")
        g_out = [sem(f"g_out{i}") for i in range(NCH)]
        s_xt = sem("s_xt")
        s_xtc = sem("s_xtc")
        s_gate = sem("s_gate")
        s_onehot = sem("s_onehot")
        s_dm = sem("s_dm")
        s_tanh = sem("s_tanh")
        s_count = sem("s_count")
        s_ohs = sem("s_ohs")
        s_inv = sem("s_inv")
        s_route = sem("s_route")
        xg_in = [sem("xg_in0"), sem("xg_in1")]
        m_xt, m_z, m_ht, m_y = (sem(n) for n in ("m_xt", "m_z", "m_ht", "m_y"))
        m_xh, m_h, m_hh = (sem(n) for n in ("m_xh", "m_h", "m_hh"))
        m_xl, m_zb, m_hl, m_yo = (sem(n) for n in ("m_xl", "m_zb", "m_hl", "m_yo"))
        m_yst = [sem("m_yst0"), sem("m_yst1")]
        dve = sem("dve")
        pool = sem("pool")
        actc = sem("actc")
        cg_in = sem("cg_in")
        yg_in = [sem(f"yg_in{i}") for i in range(4)]
        c_comb = sem("c_comb")
        x1_st = sem("x1_st")
        c_rstd, c_xn, c_xt, c_xh, c_xl = (sem(n) for n in ("c_rstd", "c_xn", "c_xt", "c_xh", "c_xl"))
        c_ab, c_th, c_sig, c_sgh, c_sgl = (sem(n) for n in ("c_ab", "c_th", "c_sig", "c_sgh", "c_sgl"))
        c_proj, c_ev, c_frac, c_trig, c_conv = (sem(n) for n in ("c_proj", "c_ev", "c_frac", "c_trig", "c_conv"))
        c_bc, c_scan, c_sq, c_sqa, c_ssq = (sem(n) for n in ("c_bc", "c_scan", "c_sq", "c_sqa", "c_ssq"))
        c_ms, c_pow, c_rb, c_root = (sem(n) for n in ("c_ms", "c_pow", "c_rb", "c_root"))
        c_norm, c_out, c_ob, c_x2 = (sem(n) for n in ("c_norm", "c_out", "c_ob", "c_x2"))
        x1t_in = [sem("x1t_in0"), sem("x1t_in1")]
        x2_st = [sem("x2_st0"), sem("x2_st1")]
        f_in, f_out, f_comb = sem("f_in"), sem("f_out"), sem("f_comb")
        zero_init = sem("zero_init")

        block = ctx.enter_context(nc.Block())

        def rows4(ap, g):
            return ap[bass.ds(g * CH, CH), :].rearrange("(a p) d -> p a d", p=P)

        @block.sync
        def _(sp):
            for dst, src in ((gw[:, :, :], gate_wT.rearrange("(k p) e -> p k e", p=P)),
                             (gb[:, :, :], gate_bias.partition_broadcast(P)),
                             (conv_sb[:, :, :, :], conv), (rms_sb[:, :], rms_w), (turns_sb[:, :], turns)):
                sp.dma_start(dst, src).then_inc(params, 16)
            for par in (0, 1):
                sp.sem_inc(m_yst[par], 1)
                sp.sem_inc(x2_st[par], 1)

            def fetch_groups(src):
                for g in range(NCH):
                    sp.dma_start(lg[:, g], rows4(src, g)).then_inc(g_in[g], 16)

            def store_groups(ph):
                for g in range(NCH):
                    sp.wait_ge(s_xn, NT * ph + TPC * (g + 1))
                    sp.dma_start(rows4(xn_rows, g), lg[:, g]).then_inc(g_out[g], 16)

            def slots(ph):
                def store(t, par):
                    sp.wait_ge(m_yo, SLOT_TILES * ph + t + 3)
                    sp.dma_start(slot_out[bass.ds(t * P, P), :], yo[:, par]).then_inc(m_yst[par], 16)

                def turn(j, pieces, keep=False):
                    if keep:
                        sp.dma_start(w_saved[bass.ds(j, 1), :, :].rearrange("a p w -> p (a w)"),
                                     wexp[:, bass.ds(j, 1), :].rearrange("p a w -> p (a w)")).then_inc(w_save, 16)
                    if pieces:
                        sp.wait_ge(a_lo, j + 1)
                        sp.dma_start(apiece, att_w[:, bass.ds(j * PIECE, PIECE)]).then_inc(a_in, 16)
                    store(2 * j, 0)
                    store(2 * j + 1, 1)

                split = 0 if ph else PIECES
                if split:
                    sp.wait_ge(s_inv, 1)
                    sp.wait_ge(w_ready, E)
                    with sp.Fori(0, E) as j:
                        turn(j, True, True)
                    with sp.Fori(E, split) as j:
                        turn(j, True)
                with sp.Fori(split, SLOT_TILES // 2) as j:
                    turn(j, False)
                store(SLOT_TILES - 1, 0)

            def outputs_stored(ph):
                for par in (0, 1):
                    sp.wait_ge(m_yst[par], 16 * (ph + 1) * (SLOT_TILES // 2 + 1 - par) + 1)

            fetch_groups(x_in)
            store_groups(0)
            slots(0)
            outputs_stored(0)

            def group_in(c):
                sp.dma_start(xgrp, rows4(x_in, c)).then_inc(cg_in, 16)

            def group_out(c):
                sp.wait_ge(c_comb, TPC * (c + 1))
                sp.dma_start(rows4(x1_rows, c), xgrp).then_inc(x1_st, 16)

            def next_group_in(c):
                sp.wait_ge(x1_st, 16 * c)
                sp.wait_ge(c_xn, TPC * c)
                group_in(c)

            def out_tiles(c):
                def fetch(i):
                    n = TPC * c + i
                    sp.wait_ge(c_x2, n + 1)
                    sp.dma_start(x1t[:, i % 2], x1_rows[bass.ds(n * P, P), :]).then_inc(x1t_in[i % 2], 16)

                def put(i):
                    n = TPC * c + i
                    sp.wait_ge(c_x2, n + 3)
                    sp.dma_start(x2_rows[bass.ds(n * P, P), :], x2t[:, i % 2]).then_inc(x2_st[i % 2], 16)

                fetch(0)
                fetch(1)
                for i in range(TPC):
                    put(i)
                    if i + 2 < TPC:
                        fetch(i + 2)

            sp.wait_ge(w_save, 16 * E)
            group_in(0)
            group_out(0)
            next_group_in(1)
            group_out(1)
            for c in range(1, NCH - 1):
                next_group_in(c + 1)
                out_tiles(c - 1)
                group_out(c + 1)
            out_tiles(NCH - 2)
            sp.wait_ge(x1_st, 16 * NCH)
            out_tiles(NCH - 1)
            for par in (0, 1):
                sp.wait_ge(x2_st[par], 16 * (NT // 2) + 1)

            fetch_groups(x2_rows)
            sp.dma_start(wexp, w_saved.rearrange("e p w -> p e w")).then_inc(w_back, 16)
            sp.dma_start(b1_bc, b1.partition_broadcast(P)).then_inc(b1_in[1], 16)
            store_groups(1)
            slots(1)
            outputs_stored(1)

            for g in range(NCH):
                if g:
                    sp.wait_ge(f_out, 16 * g)
                sp.dma_start(xgrp, rows4(x2_rows, g)).then_inc(f_in, 16)
                sp.wait_ge(f_comb, TPC * (g + 1))
                sp.dma_start(rows4(out, g), xgrp).then_inc(f_out, 16)
            sp.wait_ge(f_out, 16 * NCH)

        @block.gpsimd
        def _(gp):
            ch = Chain(gp, pool)

            def seq(ins):
                ch(ins)
                ch.wait()

            def select(out_, in_, op, fill, base, pattern, per_row):
                seq(gp.affine_select(out=out_, in_=in_, compare_op=op, fill=fill, base=base, pattern=pattern,
                                     channel_multiplier=per_row))

            def count(out_, base, pattern, per_row):
                return gp.iota(out_, pattern=pattern, base=base, channel_multiplier=per_row,
                               allow_small_or_imprecise_dtypes=True)

            for buf, value in ((ident, 0.0), (ones, 1.0), (headmean, 1.0 / P), (sel, 0.0),
                               (half_pi, PI2 / 4), (epsc, EPS), (restart, 1.0), (power, -0.5)):
                seq(gp.memset(buf.ap(), value))
            seq(gp.memset(restart[:, :, 0:1], 0.0))
            seq(gp.memset(headmean[0:64, 64:128], 0.0))
            seq(gp.memset(headmean[64:128, 0:64], 0.0))
            select(ident[:, :], ident[:, :], ALU.not_equal, 1.0, 0, [[-1, P]], 1)
            select(before[:, :], ones[:, :], ALU.is_gt, 0.0, 0, [[1, P]], -1)
            sel_rows = sel[:, :, :, :].rearrange("r t p (h c) -> r (t p h) c", h=2)
            for first in (0, 32):
                select(sel_rows, sel_rows, ALU.not_equal, 1.0, -first, [[-1, NAB], [0, 64]], 1)
            seq(count(desc[:, :, :], E, [[0, NT], [-1, E]], 0))
            seq(count(lane[:, :], 0, [[1, P]], 0))
            count(tokid[:, :], 0, [[P, NT]], 1).then_inc(consts, 1)
            gp.wait_ge(consts, 1)
            gp.dma_start(b1_bc, b1.partition_broadcast(P)).then_inc(b1_in[0], 16)
            for e in range(E):
                if e >= STAGES:
                    gp.wait_ge(w_ready, e - STAGES + 1)
                gp.dma_start(wstage[:, e % STAGES], ffn_w[e, :, :]).then_inc(w_in[e % STAGES], 16)

            def gather(dst, rows, index, done):
                gp.indirect_dma_start(dst, None, rows, bass.IndirectOffsetOnAxis(ap=index, axis=0)).then_inc(done, 16)

            def slots(ph):
                gp.wait_ge(s_route, ph + 1)
                for g in range(NCH):
                    gp.wait_ge(g_out[g], 16 * (ph + 1))
                for t in range(SLOT_TILES):
                    gp.wait_ge(m_xt, SLOT_TILES * ph + t + 1)
                    gather(xg[:, t % 2], xn_rows, slot_tok[:, t:t + 1], xg_in[t % 2])

            def fetch_outputs(c, free):
                for i in range(TPC):
                    n = TPC * c + i
                    if c:
                        gp.wait_ge(free, n - TPC + 1)
                    for k in (0, 1):
                        gather(yg[:, i, k], slot_out, pos_i[:, k, n:n + 1], yg_in[i])

            def root_of(u):
                gp.wait_ge(c_ms, u + 1)
                gp.tensor_tensor(root_, msq, power[:, :, :], ALU.pow).then_inc(c_pow, 1)

            def add_squares(u):
                gp.wait_ge(c_sq, u + 1)
                gp.wait_ge(c_ssq, u + 1)
                gp.tensor_tensor(sqa, sqs[:, 0], sqs[:, 1], ALU.add).then_inc(c_sqa, 1)

            def add_out(c):
                for i in range(TPC):
                    n, j = TPC * c + i, 2 * c + i // 2
                    gp.wait_ge(c_ob, n + 3)
                    gp.wait_ge(x1t_in[i % 2], 16 * (j + 1))
                    gp.wait_ge(x2_st[i % 2], 16 * j + 1)
                    gp.tensor_tensor(x2t[:, i % 2], ob[:, i % 2], x1t[:, i % 2], ALU.add).then_inc(c_x2, 1)

            def outputs_stored(ph):
                for par in (0, 1):
                    gp.wait_ge(m_yst[par], 16 * (ph + 1) * (SLOT_TILES // 2 + 1 - par) + 1)

            gp.sem_inc(c_x2, 2)
            gp.sem_inc(c_sqa, 1)
            slots(0)
            outputs_stored(0)
            gp.wait_ge(w_save, 16 * E)
            fetch_outputs(0, c_comb)
            for c in range(NCH):
                if c:
                    root_of(3 * c - 1)
                add_squares(3 * c)
                if c < NCH - 1:
                    fetch_outputs(c + 1, c_comb)
                root_of(3 * c)
                if c:
                    add_out(c - 1)
                add_squares(3 * c + 1)
                root_of(3 * c + 1)
                add_squares(3 * c + 2)
            root_of(3 * NCH - 1)
            add_out(NCH - 1)
            slots(1)
            outputs_stored(1)
            for g in range(NCH):
                fetch_outputs(g, f_comb)

        @block.tensor
        def _(pe):
            def transpose4(dst, src):
                for k in range(KD):
                    last = pe.transpose(dst[:, k * P:(k + 1) * P], src[:, k * P:(k + 1) * P], ident[:, :])
                return last

            def products(dst, terms):
                for n, (a, b) in enumerate(terms):
                    last = pe.matmul(dst, a, b, start=(n == 0), stop=(n == len(terms) - 1))
                return last

            def score_tiles(ph):
                o = NT * ph

                def xt(n):
                    pe.wait_ge(s_xn, o + n + 1)
                    pe.wait_ge(s_xtc, o + n + 1)
                    transpose4(bank[n % 2], lg[:, n // TPC, n % TPC]).then_inc(s_xt, 1)

                def score(n):
                    pe.wait_ge(s_xtc, o + n + 3)
                    products(bank[2][:, n * E:(n + 1) * E],
                             [(xnT[:, n % 2, k, :], gw[:, k, :]) for k in range(KD)]).then_inc(s_gate, 1)

                xt(0)
                for n in range(1, NT):
                    xt(n)
                    score(n - 1)
                score(NT - 1)

            def route(ph):
                pe.wait_ge(s_onehot, ph + 1)
                chosen = M8.rearrange("p a b -> p (a b)")
                products(bank[3][:, 0:NT * E], [(before[:, :], chosen)])
                products(bank[4][:, 0:NT * E], [(ones[:, :], chosen)]).then_inc(s_count, 1)
                pe.wait_ge(s_ohs, ph + 1)
                products(bank[5][:, 0:SLOT_TILES],
                         [(OHlo[:, k, t, :], OHhi[:, k, t, 0:SLOT_TILES]) for k in (0, 1) for t in range(NT)]).then_inc(s_inv, 1)

            def slots(ph):
                o = SLOT_TILES * ph
                g = (SLOT_TILES // 2 + 1) * ph

                def xt(t, j, par):
                    pe.wait_ge(xg_in[par], 16 * (g - par * ph + j + 1))
                    pe.wait_ge(m_xl, o + t + 1)
                    transpose4(bank[par], xg[:, par]).then_inc(m_xt, 1)

                def up(t, par):
                    ev = pe.value_load(tile_exp[0:1, bass.ds(t, 1)], min_val=0, max_val=E - 1)
                    pe.wait_ge(m_xl, o + t + 3)
                    pe.wait_ge(m_zb, o + t + 1)
                    products(bank[2 + par][:, 0:HID],
                             [(a[:, par, k * P:(k + 1) * P], w1(part, k, ev))
                              for k in range(KD) for a, part in ((xh, 0), (xh, 1), (xl, 0))]).then_inc(m_z, 1)
                    return ev

                def ht(t, par):
                    pe.wait_ge(m_h, o + t + 3)
                    pe.wait_ge(m_hl, o + t + 1)
                    for c in range(KH):
                        last = pe.transpose(bank[4 + par][:, c * P:(c + 1) * P], hact[:, par, c * P:(c + 1) * P], ident[:, :])
                    last.then_inc(m_ht, 1)

                def down(t, par):
                    ev = pe.value_load(tile_exp[0:1, bass.ds(t, 1)], min_val=0, max_val=E - 1)
                    pe.wait_ge(m_hl, o + t + 3)
                    pe.wait_ge(m_yo, o + t + 1)
                    products(bank[6 + par][:, :],
                             [(a[:, par, c, :], w2(part, c, ev)) for c in range(KH)
                              for a, part in ((hh, 0), (hh, 1), (hl, 0))]).then_inc(m_y, 1)

                pe.wait_ge(s_route, ph + 1)
                if ph == 0:
                    pe.wait_ge(w_ready, E)
                else:
                    pe.wait_ge(w_back, 16)
                xt(0, 0, 0)
                up(0, 0)
                xt(1, 0, 1)

                def step(t, j, par):
                    other = 1 - par
                    ht(t, par)
                    up(t + 1, other)
                    xt(t + 2, j + 1, par)
                    down(t, par)

                with pe.Fori(0, SLOT_TILES // 2 - 1) as j:
                    step(2 * j, j, 0)
                    step(2 * j + 1, j, 1)
                t = SLOT_TILES - 3
                step(t, t // 2, 0)
                ht(t + 1, 1)
                up(t + 2, 0)
                down(t + 1, 1)
                ht(t + 2, 0)
                down(t + 2, 0)

            def mixer_in(c, roots=None):
                for i in range(TPC):
                    n = TPC * c + i
                    pe.wait_ge(c_xn, n + 1)
                    pe.wait_ge(c_xl, n + 1)
                    if not (isinstance(c, int) and c < 2):
                        pe.wait_ge(c_ob, TPC * (c - 1) + 2)
                    if roots is not None:
                        if i == 1:
                            pe.wait_ge(c_ms, roots + 1)
                        if i == 2:
                            spread_roots(roots)
                    transpose4(bank[6 + i % 2], xnt[:, i % 2]).then_inc(c_xt, 1)
                pe.wait_ge(c_xl, TPC * (c + 1) + 2)
                products(bank[6][0:NAB, :],
                         [(att[:, part, AB0 + k * NAB:AB0 + (k + 1) * NAB], x[:, k, :])
                          for k in range(KD) for part, x in ((0, xTh), (1, xTh), (0, xTl))]).then_inc(c_ab, 1)

            def project(c, p, roots=None):
                for kind in range(KINDS):
                    m = KINDS * (PAIRS * c + p) + kind
                    col = (p * KINDS + kind) * P
                    if roots is not None and kind == 2:
                        spread_roots(roots)
                    pe.wait_ge(c_ev, m + 1)
                    products(bank[kind % 3][:, :],
                             [(att[:, part, k * NCOL + col:k * NCOL + col + P], x[:, k, :])
                              for k in range(KD) for part, x in ((0, xTh), (1, xTh), (0, xTl))]).then_inc(c_proj, 1)

            def spread(c, p):
                pe.wait_ge(c_sgl, c + 1)
                pe.wait_ge(c_scan, PAIRS * c + p + 1)
                products(bank[3][:, :], [(sel[:, 1, p, :], sigab)])
                products(bank[4][:, :], [(sel[:, 0, p, :], sigab)]).then_inc(c_bc, 1)

            def mean_square(u):
                pe.wait_ge(c_sqa, u + 2)
                for i in range(TPC):
                    last = products(bank[7][:, 2 * i:2 * i + 2], [(sqa[:, i * P:(i + 1) * P], heads)])
                last.then_inc(c_ssq, 1)

            def spread_roots(u):
                pe.wait_ge(c_rb, u + 1)
                pe.wait_ge(c_norm, u + 3)
                for i in range(TPC):
                    last = products(bank[5][:, i * P:(i + 1) * P],
                                    [(rootb[:, i].rearrange("p h c -> p (h c)"), ident[:, :])])
                last.then_inc(c_root, 1)

            def project_out(c, split, roots):
                pe.wait_ge(c_norm, PAIRS * (c + 1) + 3)
                pe.wait_ge(c_xl, split)
                pe.wait_ge(c_th, c + 1)
                for i in range(TPC):
                    pe.wait_ge(c_ob, TPC * c + i + 1)
                    if i == 1 and roots is not None:
                        spread_roots(roots)
                    products(bank[6 + i % 2][:, :],
                             [(a[:, r, i * P:(i + 1) * P], att[:, part, WO0 + r * D:WO0 + (r + 1) * D])
                              for r in range(2 * PAIRS) for a, part in ((oh, 0), (oh, 1), (ol, 0))]).then_inc(c_out, 1)

            def chunk(c, first, last):
                project(c, 0)
                spread(c, 0)
                if not first:
                    mean_square(3 * c - 1)
                project(c, 1, None if first else 3 * c - 1)
                spread(c, 1)
                mean_square(3 * c)
                if not first:
                    project_out(c - 1, TPC * (c + 1) + 2, 3 * c)
                project(c, 2, 3 * c if first else None)
                spread(c, 2)
                if not first:
                    pe.wait_ge(c_ob, TPC * c + 2)
                mean_square(3 * c + 1)
                if not last:
                    mixer_in(c + 1, 3 * c + 1)

            heads = headmean[:, :].rearrange("p (h c) -> p h c", h=2)[:, :, 0]
            for s, n in ((s_gate, 2), (m_xt, 2), (m_z, 2), (m_ht, 2), (m_y, 2), (c_xt, 2), (c_ssq, 1), (c_out, 1), (c_root, 1)):
                pe.sem_inc(s, n)
            pe.wait_ge(consts, 1)
            pe.wait_ge(params, 16 * 5)
            score_tiles(0)
            route(0)
            slots(0)
            pe.wait_ge(a_lo, PIECES + 1)
            mixer_in(0)
            chunk(0, True, False)
            with pe.Fori(1, NCH - 1) as c:
                chunk(c, False, False)
            chunk(NCH - 1, False, True)
            spread_roots(3 * NCH - 2)
            mean_square(3 * NCH - 1)
            spread_roots(3 * NCH - 1)
            project_out(NCH - 1, NT + 2, None)
            score_tiles(1)
            route(1)
            slots(1)

        @block.scalar
        def _(act):
            ch = Chain(act, actc)

            def split_high(e):
                act.wait_ge(w_in[e % STAGES], 16 * (e // STAGES + 1))
                act.activation(wexp[:, e, 0:FW], wstage[:, e % STAGES], ACT.Copy, scale=WSCALE).then_inc(w_hi, 1)

            def normalise_groups(ph):
                o = NT * ph
                for g in range(NCH):
                    act.wait_ge(s_rstd, NCH * ph + g + 1)
                    for i in range(TPC):
                        act.activation(lg[:, g, i], lg[:, g, i], ACT.Identity, scale=rstd[:, g, 0, i:i + 1],
                                       bias=rstd[:, g, 1, i:i + 1]).then_inc(s_xn, 1)
                    for n in range(TPC * g, TPC * (g + 1)):
                        act.wait_ge(s_xt, o + n + 1)
                        act.wait_ge(s_gate, o + n + 1)
                        act.activation(xnT[:, n % 2].rearrange("p k c -> p (k c)"), bank[n % 2][:, :], ACT.Copy).then_inc(s_xtc, 1)
                    if ph == 0:
                        split_high(g)

            def slots(ph):
                o = SLOT_TILES * ph

                def x_high(t, par):
                    act.wait_ge(m_xt, o + t + 3)
                    act.wait_ge(m_z, o + t + 1)
                    act.activation(xh[:, par], bank[par][:, :], ACT.Copy).then_inc(m_xh, 1)

                def silu(t, par):
                    act.wait_ge(m_zb, o + t + 3)
                    act.wait_ge(m_ht, o + t + 1)
                    act.activation(hact[:, par, 0:HID], z[:, par], ACT.Silu).then_inc(m_h, 1)

                def h_high(t, par):
                    act.wait_ge(m_ht, o + t + 3)
                    act.wait_ge(m_y, o + t + 1)
                    act.activation(hh[:, par].rearrange("p a b -> p (a b)"), bank[4 + par][:, 0:KH * P], ACT.Copy).then_inc(m_hh, 1)

                def piece(q):
                    act.wait_ge(a_in, 16 * (q + 1))
                    act.activation(att[:, 0, bass.ds(q * PIECE, PIECE)], apiece, ACT.Copy, scale=WSCALE).then_inc(a_hi, 1)

                def step(t, par):
                    h_high(t, par)
                    silu(t + 1, 1 - par)
                    x_high(t + 2, par)

                if ph == 0:
                    act.wait_ge(w_ready, E)
                x_high(0, 0)
                silu(0, 0)
                x_high(1, 1)
                split = 0 if ph else PIECES
                if split:
                    with act.Fori(0, split) as j:
                        step(2 * j, 0)
                        step(2 * j + 1, 1)
                        piece(j)
                with act.Fori(split, SLOT_TILES // 2 - 1) as j:
                    step(2 * j, 0)
                    step(2 * j + 1, 1)
                t = SLOT_TILES - 3
                step(t, 0)
                h_high(t + 1, 1)
                silu(t + 2, 0)
                h_high(t + 2, 0)

            def normalise(c, i):
                act.wait_ge(c_rstd, c + 1)
                act.wait_ge(c_xt, TPC * c + i + 1)
                act.activation(xnt[:, i % 2], xgrp[:, i], ACT.Identity, scale=rstd[:, 0, 0, i:i + 1],
                               bias=rstd[:, 0, 1, i:i + 1]).then_inc(c_xn, 1)

            def x_high(c, i):
                act.wait_ge(c_xt, TPC * c + i + 3)
                act.activation(xTh[:, :, i * P:(i + 1) * P], bank[6 + i % 2][:, :].rearrange("p (k c) -> p k c", k=KD),
                               ACT.Copy).then_inc(c_xh, 1)

            def chunk_in(c):
                for i in range(TPC):
                    x_high(c, i)
                    if i + 2 < TPC:
                        normalise(c, i + 2)
                act.wait_ge(c_ab, c + 1)
                act.activation(abt[0:NAB], bank[6][0:NAB, :], ACT.Tanh, scale=0.5 * UNSCALE).then_inc(c_th, 1)
                act.wait_ge(c_sig, c + 1)
                if not (isinstance(c, int) and c == 0):
                    act.wait_ge(c_bc, PAIRS * c)
                act.activation(sigab[0:NAB], abs_[0:NAB], ACT.Copy).then_inc(c_sgh, 1)

            def evacuate(c, p, kinds):
                u = PAIRS * c + p
                for kind in kinds:
                    act.wait_ge(c_proj, KINDS * u + kind + 1)
                    if kind < 4:
                        act.wait_ge(c_conv, u + 1)
                        act.activation(raw[:, p, kind, HALO:], bank[kind % 3][:, :], ACT.Copy, scale=UNSCALE).then_inc(c_ev, 1)
                    else:
                        act.wait_ge(c_norm, u + 1)
                        act.activation(sg[:, p, kind - 4], bank[kind % 3][:, :], ACT.Silu, scale=UNSCALE).then_inc(c_ev, 1)

            def trig(u):
                act.wait_ge(c_frac, u + 1)
                act.activation(sn, frac, ACT.Sin, scale=PI2)
                ch(act.activation(af, frac, ACT.Abs))
                ch.wait()
                act.activation(cs, af, ACT.Sin, scale=-PI2, bias=half_pi[:, 0:1]).then_inc(c_trig, 1)

            def root(u):
                act.wait_ge(c_ssq, u + 2)
                act.activation(msq.rearrange("p a b -> p (a b)"), bank[7][:, 0:2 * TPC], ACT.Identity,
                               bias=epsc[:, 0:1]).then_inc(c_ms, 1)
                act.wait_ge(c_pow, u + 1)
                act.wait_ge(c_root, u + 1)
                act.activation(rootb, root_.unsqueeze(3).to_broadcast([P, TPC, 2, P // 2]), ACT.Copy).then_inc(c_rb, 1)

            def squares(u):
                act.wait_ge(c_scan, u + 2)
                act.wait_ge(c_sqa, u + 1)
                for eo in (0, 1):
                    last = act.activation(sqs[:, eo], res[:, u_pair[0], eo], ACT.Square)
                last.then_inc(c_sq, 1)

            u_pair = [0]

            def chunk(n, c, first, last):
                allk = range(KINDS)
                evacuate(c, 1, (0, 1))
                trig(3 * c)
                if not first:
                    root(3 * c - 1)
                evacuate(c, 1, (2, 3, 4, 5))
                u_pair[0] = 0
                squares(3 * c)
                trig(3 * c + 1)
                root(3 * c)
                if not first:
                    out_tiles(c - 1)
                evacuate(c, 2, allk)
                u_pair[0] = 1
                squares(3 * c + 1)
                if not last:
                    normalise(c + 1, 0)
                    normalise(c + 1, 1)
                trig(3 * c + 2)
                root(3 * c + 1)
                if not last:
                    chunk_in(c + 1)
                    evacuate(c + 1, 0, allk)
                u_pair[0] = 2
                squares(3 * c + 2)

            def out_tiles(c):
                for i in range(TPC):
                    n = TPC * c + i
                    act.wait_ge(c_out, n + 2)
                    act.wait_ge(c_x2, n + 1)
                    act.activation(ob[:, i % 2], bank[6 + i % 2][:, :], ACT.Copy, scale=UNSCALE).then_inc(c_ob, 1)

            for s, n in ((s_xtc, 2), (m_h, 2), (c_ev, 3), (c_ob, 2)):
                act.sem_inc(s, n)
            act.wait_ge(consts, 1)
            normalise_groups(0)
            act.wait_ge(s_dm, 1)
            act.activation(th, dm, ACT.Tanh, scale=0.5).then_inc(s_tanh, 1)
            for e in range(NCH, E):
                split_high(e)
            slots(0)
            normalise(0, 0)
            normalise(0, 1)
            chunk_in(0)
            evacuate(0, 0, range(KINDS))
            chunk(0, 0, True, False)
            ch.loop(1, NCH - 1, 3, lambda c: chunk(None, c, False, False))
            chunk(None, NCH - 1, False, True)
            root(3 * NCH - 1)
            out_tiles(NCH - 1)
            normalise_groups(1)
            act.wait_ge(s_dm, 2)
            act.activation(th, dm, ACT.Tanh, scale=0.5).then_inc(s_tanh, 1)
            slots(1)

        @block.vector
        def _(v):
            ch = Chain(v, dve)

            def seq(ins):
                ch(ins)
                ch.wait()

            def inv_std(par, done):
                a, y, t1 = nt4[:, 0], nt4[:, 1], nt4[:, 2]
                ch(v.tensor_tensor(mv[:, :, 0], bst[:, :, 1], bst[:, :, 4], ALU.add))
                ch(v.tensor_tensor(mv[:, :, 1], bst[:, :, 1], bst[:, :, 4], ALU.subtract))
                seq(v.tensor_tensor(a, bst[:, :, 2], bst[:, :, 5], ALU.add))
                ch(v.scalar_tensor_tensor(t1, mv[:, :, 1], 0.25, mv[:, :, 1], ALU.mult, ALU.mult))
                seq(v.tensor_scalar(a, a, 1.0 / D, EPS, ALU.mult, ALU.add))
                seq(v.tensor_tensor(a, a, t1, ALU.add))
                seq(v.tensor_scalar(y.bitcast(I32), a.bitcast(I32), -0.5, RSQRT_SEED, ALU.mult, ALU.add))
                for _ in range(3):
                    seq(v.tensor_tensor(t1, y, y, ALU.mult))
                    seq(v.scalar_tensor_tensor(t1, t1, -0.5, a, ALU.mult, ALU.mult))
                    seq(v.scalar_tensor_tensor(y, t1, 1.5, y, ALU.add, ALU.mult))
                v.tensor_copy(rstd[:, par, 0], y)
                v.scalar_tensor_tensor(rstd[:, par, 1], mv[:, :, 0], -0.5, y, ALU.mult, ALU.mult).then_inc(done, 1)

            def stats(rows):
                for i in range(TPC):
                    ch(v.bn_stats(bst[:, i], rows[:, i]))
                ch.wait()

            def split_low(e):
                v.wait_ge(w_hi, e + 1)
                v.scalar_tensor_tensor(wexp[:, e, FW:2 * FW], wstage[:, e % STAGES], WSCALE, wexp[:, e, 0:FW],
                                       ALU.mult, ALU.subtract).then_inc(w_ready, 1)

            def group_stats(ph):
                for g in range(NCH):
                    v.wait_ge(g_in[g], 16 * (ph + 1))
                    stats(lg[:, g])
                    inv_std(g, s_rstd)
                if ph == 0:
                    for e in range(NCH):
                        split_low(e)

            def round_down(dst, src, tmp_):
                seq(v.tensor_scalar(tmp_, src, -63.5, 1.0 / P, ALU.add, ALU.mult))
                seq(v.tensor_scalar(dst, tmp_, MAGIC, MAGIC, ALU.add, ALU.subtract))

            def route(ph):
                def bc(x):
                    return x.unsqueeze(2).to_broadcast([P, NT, E])

                def eb(x):
                    return x.unsqueeze(2).to_broadcast([P, E, NT])

                flat = "p a b -> p (a b)"
                v.wait_ge(s_gate, NT * (ph + 1) + 2)
                if ph == 0:
                    seq(v.tensor_tensor(gb[:, 0], gb[:, 0], gb[:, 1], ALU.add))
                seq(v.tensor_tensor(S, bank[2][:, 0:NT * E].rearrange("p (a b) -> p a b", b=E),
                                    gb[:, 0].unsqueeze(1).to_broadcast([P, NT, E]), ALU.add))
                seq(v.reduce_max(m1, S, AX))
                seq(v.tensor_tensor(KEY, S, bc(m1), ALU.is_equal))
                seq(v.tensor_tensor(KEY, KEY, desc[:, :, :], ALU.mult))
                seq(v.reduce_max(k1, KEY, AX))
                seq(v.tensor_tensor(OH1, desc[:, :, :], bc(k1), ALU.is_equal))
                seq(v.scalar_tensor_tensor(S2.rearrange(flat), OH1.rearrange(flat), 0.0, S.rearrange(flat), ALU.is_equal, ALU.mult))
                seq(v.scalar_tensor_tensor(S2.rearrange(flat), OH1.rearrange(flat), -3.0e38, S2.rearrange(flat), ALU.mult, ALU.add))
                seq(v.reduce_max(k1, S2, AX))
                v.tensor_tensor(dm, k1, m1, ALU.subtract).then_inc(s_dm, 1)
                seq(v.tensor_tensor(KEY, S2, bc(k1), ALU.is_equal))
                seq(v.tensor_tensor(KEY, KEY, desc[:, :, :], ALU.mult))
                seq(v.reduce_max(k1, KEY, AX))
                seq(v.tensor_tensor(OH2, desc[:, :, :], bc(k1), ALU.is_equal))
                v.tensor_tensor(M8, OH1, OH2, ALU.add).then_inc(s_onehot, 1)
                if ph == 0:
                    split_low(NCH)
                    split_low(NCH + 1)
                v.wait_ge(s_tanh, ph + 1)
                v.tensor_scalar(ghalf[:, 0], th, -0.25, 0.25, ALU.mult, ALU.add)
                v.tensor_scalar(ghalf[:, 1], th, 0.25, 0.25, ALU.mult, ALU.add)
                seq(v.memset(one8, 1.0))
                v.wait_ge(s_count, ph + 1)
                seq(v.tensor_copy(CE, bank[4][:, 0:NT * E].rearrange("p (t e) -> p e t", e=E)))
                seq(v.tensor_tensor_scan(SC.rearrange(flat), restart[:, :, :].rearrange(flat), CE.rearrange(flat), 0.0, ALU.mult, ALU.add))
                ch(v.tensor_tensor(EX, SC, CE, ALU.subtract))
                seq(v.tensor_scalar(tl, SC[:, :, NT - 1], float(P - 1), None, ALU.add))
                round_down(tl, tl, st8)
                seq(v.tensor_tensor_scan(en, one8, tl, 0.0, ALU.mult, ALU.add))
                seq(v.tensor_tensor(st8, en, tl, ALU.subtract))
                seq(v.tensor_scalar(base8, st8, float(P), None, ALU.mult))
                seq(v.tensor_tensor(EX, EX, eb(base8), ALU.add))
                seq(v.tensor_tensor(QP, bank[3][:, 0:NT * E].rearrange("p (a b) -> p a b", b=E),
                                    EX.rearrange("p e t -> p t e"), ALU.add))
                for k, oh_ in ((0, OH1), (1, OH2)):
                    seq(v.tensor_tensor(KEY, QP, oh_, ALU.mult))
                    seq(v.reduce_sum(posf[:, k], KEY, AX))
                ch(v.tensor_copy(pos_i[:, :, :], posf))
                round_down(hi_f, posf, lo_f)
                for g in range(NCH):
                    v.wait_ge(g_out[g], 16 * (ph + 1))
                seq(v.scalar_tensor_tensor(lo_f, hi_f, -float(P), posf, ALU.mult, ALU.add))
                for k in (0, 1):
                    ch(v.tensor_tensor(OHlo[:, k], lo_f[:, k].unsqueeze(2).to_broadcast([P, NT, P]),
                                       lane[:, :].unsqueeze(1).to_broadcast([P, NT, P]), ALU.is_equal))
                    seq(v.tensor_tensor(OHhi[:, k, :, 0:SLOT_TILES], hi_f[:, k].unsqueeze(2).to_broadcast([P, NT, SLOT_TILES]),
                                        lane[:, 0:SLOT_TILES].unsqueeze(1).to_broadcast([P, NT, SLOT_TILES]), ALU.is_equal))
                    last = v.tensor_tensor(OHhi[:, k, :, 0:SLOT_TILES], OHhi[:, k, :, 0:SLOT_TILES],
                                           tokid[:, :].unsqueeze(2).to_broadcast([P, NT, SLOT_TILES]), ALU.mult)
                    if k == 0:
                        ch(last)
                last.then_inc(s_ohs, 1)
                seq(v.tensor_tensor(cmp, lane[:, 0:SLOT_TILES].unsqueeze(2).to_broadcast([P, SLOT_TILES, E]),
                                    en.unsqueeze(1).to_broadcast([P, SLOT_TILES, E]), ALU.is_ge))
                seq(v.reduce_sum(evf, cmp, AX))
                seq(v.tensor_scalar(tile_exp[:, :], evf, float(E - 1), None, ALU.min))
                if ph == 0:
                    split_low(E - 2)
                    split_low(E - 1)
                v.wait_ge(s_inv, ph + 1)
                v.tensor_copy(slot_tok[:, :], bank[5][:, 0:SLOT_TILES]).then_inc(s_route, 1)

            def slots(ph):
                o = SLOT_TILES * ph

                def x_low(t, par):
                    v.wait_ge(m_xh, o + t + 1)
                    v.tensor_tensor(xl[:, par], bank[par][:, :], xh[:, par], ALU.subtract).then_inc(m_xl, 1)

                def add_bias(t, par):
                    ev = v.value_load(tile_exp[0:1, bass.ds(t, 1)], min_val=0, max_val=E - 1)
                    v.wait_ge(m_z, o + t + 3)
                    v.wait_ge(m_h, o + t + 1)
                    v.scalar_tensor_tensor(z[:, par], bank[2 + par][:, 0:HID], UNSCALE, b1_bc[:, bass.ds(ev * HID, HID)],
                                           ALU.mult, ALU.add).then_inc(m_zb, 1)

                def h_low(t, par):
                    v.wait_ge(m_hh, o + t + 1)
                    v.tensor_tensor(hl[:, par].rearrange("p a b -> p (a b)"), bank[4 + par][:, 0:KH * P],
                                    hh[:, par].rearrange("p a b -> p (a b)"), ALU.subtract).then_inc(m_hl, 1)

                def y_out(t, j, par):
                    v.wait_ge(m_y, o + t + 3)
                    v.wait_ge(m_yst[par], 16 * ((SLOT_TILES // 2 + 1 - par) * ph + j) + 1)
                    v.tensor_scalar(yo[:, par], bank[6 + par][:, :], UNSCALE, None, ALU.mult).then_inc(m_yo, 1)

                def piece(q):
                    v.wait_ge(a_hi, q + 1)
                    v.scalar_tensor_tensor(att[:, 1, bass.ds(q * PIECE, PIECE)], apiece, WSCALE,
                                           att[:, 0, bass.ds(q * PIECE, PIECE)], ALU.mult, ALU.subtract).then_inc(a_lo, 1)

                def step(t, j, par):
                    h_low(t, par)
                    add_bias(t + 1, 1 - par)
                    x_low(t + 2, par)
                    y_out(t, j, par)

                v.memset(hact[:, :, HID:HID + 1], 1.0)
                seq(v.memset(hact[:, :, HID + 1:KH * P], 0.0))
                v.wait_ge(b1_in[ph], 16)
                x_low(0, 0)
                add_bias(0, 0)
                x_low(1, 1)
                split = 0 if ph else PIECES
                if split:
                    with v.Fori(0, split) as j:
                        step(2 * j, j, 0)
                        step(2 * j + 1, j, 1)
                        piece(j)
                with v.Fori(split, SLOT_TILES // 2 - 1) as j:
                    step(2 * j, j, 0)
                    step(2 * j + 1, j, 1)
                t = SLOT_TILES - 3
                step(t, t // 2, 0)
                h_low(t + 1, 1)
                add_bias(t + 2, 0)
                y_out(t + 1, t // 2, 1)
                h_low(t + 2, 0)
                y_out(t + 2, t // 2 + 1, 0)

            def combine(g, arrived, uses, done):
                v.wait_ge(arrived, 16 * (g + 1))
                for i in range(TPC):
                    n = TPC * g + i
                    v.wait_ge(yg_in[i], 32 * (uses + g + 1))
                    seq(v.scalar_tensor_tensor(xgrp[:, i], yg[:, i, 0], ghalf[:, 0, bass.ds(n, 1)], xgrp[:, i], ALU.mult, ALU.add))
                    v.scalar_tensor_tensor(xgrp[:, i], yg[:, i, 1], ghalf[:, 1, bass.ds(n, 1)], xgrp[:, i], ALU.mult, ALU.add).then_inc(done, 1)

            def chunk_stats(c):
                combine(c, cg_in, 0, c_comb)
                v.wait_ge(c_comb, TPC * (c + 1))
                stats(xgrp)
                inv_std(0, c_rstd)

            def chunk_low(c):
                for i in range(TPC):
                    v.wait_ge(c_xh, TPC * c + i + 1)
                    v.tensor_tensor(xTl[:, :, i * P:(i + 1) * P], bank[6 + i % 2][:, :].rearrange("p (k c) -> p k c", k=KD),
                                    xTh[:, :, i * P:(i + 1) * P], ALU.subtract).then_inc(c_xl, 1)
                v.wait_ge(c_th, c + 1)
                v.tensor_scalar(abs_[0:NAB], abt[0:NAB], 0.5, 0.5, ALU.mult, ALU.add).then_inc(c_sig, 1)
                v.wait_ge(c_sgh, c + 1)
                v.tensor_tensor(sigab[32:32 + NAB], abs_[0:NAB], sigab[0:NAB], ALU.subtract).then_inc(c_sgl, 1)

            def angles(c, p):
                u = PAIRS * c + p
                v.wait_ge(c_ev, KINDS * u + 2 + 3)
                seq(v.tensor_scalar(ang, raw[:, p, 0, 0:CH], cang[:, p, 0, 0:1], None, ALU.mult))
                for kind, j in [(0, 1), (0, 2), (0, 3), (1, 0), (1, 1), (1, 2), (1, 3)]:
                    seq(v.scalar_tensor_tensor(ang, raw[:, p, kind, j:j + CH], cang[:, p, kind, j:j + 1], ang, ALU.mult, ALU.add))
                seq(v.tensor_scalar(rnd, ang, MAGIC, MAGIC, ALU.add, ALU.subtract))
                v.tensor_tensor(frac, ang, rnd, ALU.subtract).then_inc(c_frac, 1)
                v.wait_ge(c_ev, KINDS * u + 4 + 3)
                for eo in (0, 1):
                    ch(v.tensor_scalar(vcon[:, eo], raw[:, p, 2 + eo, 0:CH], conv_sb[:, p, 2 + eo, 0:1], None, ALU.mult))
                for j in range(1, TAPS):
                    for eo in (0, 1):
                        ch.wait(ch.n - 1)
                        ch(v.scalar_tensor_tensor(vcon[:, eo], raw[:, p, 2 + eo, j:j + CH], conv_sb[:, p, 2 + eo, j:j + 1],
                                                  vcon[:, eo], ALU.mult, ALU.add))
                ch.wait()
                v.tensor_copy(raw[:, p, :, 0:HALO], raw[:, p, :, CH:CH + HALO]).then_inc(c_conv, 1)

            def recur(c, p):
                u = PAIRS * c + p
                v.wait_ge(c_trig, u + 1)
                v.wait_ge(c_bc, u + 1)
                ch(v.tensor_tensor(sn, bank[3][:, :], sn, ALU.mult))
                ch(v.tensor_tensor(cs, bank[3][:, :], cs, ALU.mult))
                ch.wait()
                ch(v.tensor_tensor(tmp[:, 0], vcon[:, 0], cs, ALU.mult))
                ch(v.tensor_tensor(tmp[:, 1], vcon[:, 1], sn, ALU.mult))
                ch(v.tensor_tensor(tmp[:, 2], vcon[:, 1], cs, ALU.mult))
                ch(v.tensor_tensor(tmp[:, 3], vcon[:, 0], sn, ALU.mult))
                ch.wait(ch.n - 2)
                ch(v.tensor_tensor(tmp[:, 0], tmp[:, 0], tmp[:, 1], ALU.subtract))
                ch.wait(ch.n - 1)
                ch(v.tensor_tensor(tmp[:, 2], tmp[:, 2], tmp[:, 3], ALU.add))
                ch.wait(ch.n - 1)
                v.tensor_tensor_scan(res[:, p, 0], bank[4][:, :], tmp[:, 0], carry[:, p, 0:1], ALU.mult, ALU.add)
                ch.wait()
                v.tensor_tensor_scan(res[:, p, 1], bank[4][:, :], tmp[:, 2], carry[:, p, 1:2], ALU.mult, ALU.add).then_inc(c_scan, 1)
                v.wait_ge(c_scan, u + 2)
                seq(v.tensor_copy(carry[:, p, :], res[:, p, :, CH - 1]))

            def gate(c, p):
                u = PAIRS * c + p
                v.wait_ge(c_root, u + 2)
                v.wait_ge(c_ev, KINDS * (u + 1) + 3)
                v.wait_ge(c_out, TPC * c + 1)
                for eo in (0, 1):
                    ch(v.scalar_tensor_tensor(on[:, eo], res[:, p, eo], rms_sb[:, eo:eo + 1], bank[5][:, :], ALU.mult, ALU.mult))
                for eo in (0, 1):
                    ch.wait(ch.n - 1)
                    ch(v.tensor_tensor(on[:, eo], on[:, eo], sg[:, p, eo], ALU.mult))
                for eo in (0, 1):
                    ch.wait(ch.n - 1)
                    ch(v.tensor_copy(oh[:, 2 * p + eo], on[:, eo]))
                ch.wait(ch.n - 1)
                v.tensor_tensor(ol[:, 2 * p], on[:, 0], oh[:, 2 * p], ALU.subtract)
                ch.wait()
                v.tensor_tensor(ol[:, 2 * p + 1], on[:, 1], oh[:, 2 * p + 1], ALU.subtract).then_inc(c_norm, 1)

            def chunk(c, first, last):
                angles(c, 0)
                recur(c, 0)
                if not first:
                    gate(c - 1, 2)
                angles(c, 1)
                recur(c, 1)
                gate(c, 0)
                if not last:
                    chunk_stats(c + 1)
                angles(c, 2)
                if not last:
                    chunk_low(c + 1)
                recur(c, 2)
                gate(c, 1)

            for s, n in ((m_xl, 2), (m_zb, 2), (m_hl, 2), (m_yo, 2), (a_lo, 1), (c_xl, 2),
                         (c_conv, 3), (c_norm, 3), (c_scan, 1)):
                v.sem_inc(s, n)
            group_stats(0)
            v.wait_ge(consts, 1)
            v.wait_ge(params, 16 * 5)
            route(0)
            for p in range(PAIRS):
                for kind in (0, 1):
                    ch(v.tensor_scalar(cang[:, p, kind], conv_sb[:, p, kind], turns_sb[:, kind:kind + 1], None, ALU.mult))
            slots(0)
            for par in (0, 1):
                v.wait_ge(m_yst[par], 16 * (SLOT_TILES // 2 + 1 - par) + 1)
            v.wait_ge(w_save, 16 * E)
            v.memset(raw[:, :, :, 0:HALO], 0.0)
            v.memset(carry, 0.0)
            seq(v.memset(sigab, 0.0))
            chunk_stats(0)
            chunk_low(0)
            chunk(0, True, False)
            ch.loop(1, NCH - 1, CHUNK_STEPS, lambda c: chunk(c, False, False))
            chunk(NCH - 1, False, True)
            gate(NCH - 1, 2)
            group_stats(1)
            route(1)
            slots(1)
            for g in range(NCH):
                combine(g, f_in, NCH, f_comb)


def kernel(**inputs):
    import concourse.bacc as bacc
    from concourse.bass_utils import run_bass_kernel_spmd as run

    def given(name):
        return np.asarray(inputs["L0_" + name])

    w1 = given("ffn_w1").transpose(2, 0, 1).reshape(KD, P, E, HID).transpose(2, 1, 0, 3).reshape(E, P, KD * HID)
    w2 = np.zeros((E, KH * P, D), np.float32)
    w2[:, 0:HID] = given("ffn_w2").transpose(0, 2, 1)
    w2[:, HID] = given("ffn_b2")
    w2 = w2.reshape(E, KH, P, D).transpose(0, 2, 1, 3).reshape(E, P, KH * D)

    def pairs(w, eo):
        return w[:, eo::2].reshape(w.shape[0], PAIRS, 1, P)

    wq, wk, wv, wg = (given("attn_" + n) for n in ("Wq", "Wk", "Wv", "Wg"))
    cols = np.concatenate([pairs(wq, 0), pairs(wk, 0), pairs(wv, 0), pairs(wv, 1), pairs(wg, 0), pairs(wg, 1)], 2)
    ab = np.concatenate([given("attn_Wa"), given("attn_Wb")], 1)
    wo = given("attn_Wo").reshape(PAIRS, P, 2, D).transpose(1, 0, 2, 3)
    att_w = np.concatenate([cols.reshape(KD, P, NCOL).transpose(1, 0, 2).reshape(P, -1),
                            ab.reshape(KD, P, NAB).transpose(1, 0, 2).reshape(P, -1), wo.reshape(P, -1)], 1)
    cq, ck, cv = (given("attn_conv_" + n).reshape(PAIRS, P, 2, TAPS) for n in "qkv")
    conv = np.stack([cq[:, :, 0], ck[:, :, 0], cv[:, :, 0], cv[:, :, 1]], 2).transpose(1, 0, 2, 3)
    rms = given("attn_rms_w").reshape(64, 2)
    freq = 1.0 / 10000.0 ** (np.arange(0, P, 2, dtype=np.float32) / P)
    turn = np.tile(freq / (2 * np.pi), 2)
    arrays = {
        "x_in": given("attn_hidden_states").reshape(T, D),
        "ffn_w": np.concatenate([w1, w2], 2),
        "gate_wT": given("ffn_gate_w").T,
        "gate_bias": np.stack([given("ffn_gate_b"), given("ffn_bias")]),
        "b1": given("ffn_b1").reshape(E * HID),
        "att_w": att_w,
        "conv": conv,
        "rms_w": np.concatenate([rms, rms]),
        "turns": np.stack([-turn, turn], 1).astype(np.float32),
    }
    arrays = {k: np.ascontiguousarray(a) for k, a in arrays.items()}
    nc = bacc.Bacc("TRN2", target_bir_lowering=False, num_devices=1)
    args = [nc.dram_tensor(k, a.shape, mybir.dt.from_np(a.dtype), kind="ExternalInput").ap() for k, a in arrays.items()]
    out = nc.dram_tensor("out", (T, D), F32, kind="ExternalOutput").ap()
    build(nc, *args, out)
    r = run(nc, [arrays], core_ids=[0])
    return r.results[0]["out"].reshape(1, T, D)
```

```python
from contextlib import ExitStack

import numpy as np

import concourse.bass as bass
from concourse import mybir

F32, F16, I32 = mybir.dt.float32, mybir.dt.float16, mybir.dt.int32
ACT = mybir.ActivationFunctionType
ALU = mybir.AluOpType
AX = mybir.AxisListType.X

P = 128
T, D = 2048, 512
E, HID = 8, 352
NT = T // P
KD = D // P
KH = 3
LAST = HID - 2 * P
SLOT_TILES = (2 * T + E * (P - 1)) // P
FW = KD * HID + KH * D
HEADS = 6
PAIRS = HEADS // 2
KINDS = 6
TAPS = 4
CH = 512
NCH = T // CH
TPC = CH // P
HALO = TAPS - 1
NCOL = PAIRS * KINDS * P
NAB = 2 * HEADS
BLOCK = 1024
PIECES = (KD * NCOL + 2 * PAIRS * D) // BLOCK
OWN = 4
PIECE = BLOCK + NAB
STAGES = 3
WSCALE = 256.0
UNSCALE = 1.0 / WSCALE
EPS = 1e-5
MAGIC = 12582912.0
RSQRT_SEED = float(0x5F3759DF)
PI2 = float(2 * np.pi)
LAST_BANKS = (6, 3, 4, 7)
CHUNK_STEPS = 102


class Chain:

    def __init__(self, eng, sem):
        self.eng, self.sem, self.base, self.n = eng, sem, 0, 0

    def __call__(self, ins):
        self.n += 1
        ins.then_inc(self.sem, 1)
        return self.n

    def wait(self, token=None):
        self.eng.wait_ge(self.sem, self.base + (self.n if token is None else token))

    def loop(self, lo, hi, per, body):
        start, self.n = self.base + self.n, 0
        with self.eng.Fori(lo, hi) as i:
            self.base = start + (i - lo) * per
            body(i)
            assert self.n == per, (self.n, per)
        self.base, self.n = start + (hi - lo) * per, 0


def build(nc, x_in, ffn_w, gate_wT, gate_bias, b1, att_w, conv, rms_w, turns, out):
    ctx = ExitStack()
    with ctx:
        def sb(name, shape, dt=F32):
            return ctx.enter_context(nc.sbuf_tensor(name, shape, dt))

        def sem(name):
            return ctx.enter_context(nc.semaphore(name))

        def dram(name, shape, dt=F32):
            return nc.dram_tensor(name, shape, dt).ap()

        xn_rows = dram("xn_rows", (T, D))
        slot_out = dram("slot_out", (SLOT_TILES * P, D))
        x1_rows = dram("x1_rows", (T, D))
        x2_rows = dram("x2_rows", (T, D))
        w_saved = dram("w_saved", (E, P, 2 * FW), F16)

        ident = sb("ident", [P, P])
        ones = sb("ones", [P, P])
        before = sb("before", [P, P])
        headmean = sb("headmean", [P, P])
        sel = sb("sel", [44, 2, PAIRS, P], F16)
        desc = sb("desc", [P, NT, E])
        lane = sb("lane", [P, P])
        tokid = sb("tokid", [P, NT])
        lane16 = sb("lane16", [P, P], F16)
        tokid16 = sb("tokid16", [P, NT], F16)
        power = sb("power", [P, TPC, 2])
        restart = sb("restart", [P, E, NT])
        half_pi = sb("half_pi", [P, 1])
        epsc = sb("epsc", [P, 1])
        conv_sb = sb("conv_sb", [P, PAIRS, 4, TAPS])
        cang = sb("cang", [P, PAIRS, 2, TAPS])
        rms_sb = sb("rms_sb", [P, 2])
        turns_sb = sb("turns_sb", [P, 2])
        gw = sb("gw", [P, KD, E])
        gb = sb("gb", [P, 2, E])
        pos_i = sb("pos_i", [P, 2, NT], I32)
        ghalf = sb("ghalf", [P, 2, NT])
        slot_tok = sb("slot_tok", [P, SLOT_TILES], I32)
        tile_exp = sb("tile_exp", [P, SLOT_TILES], I32)
        mv = sb("mv", [P, TPC, 2])
        bst = sb("bst", [P, TPC, 6])
        nt4 = sb("nt4", [P, 4, TPC])
        rstd = sb("rstd", [P, NCH, 2, TPC])

        ATT = PIECES * PIECE
        ARENA = 38800
        space = sb("space", [P, ATT + ARENA])
        att = space[:, 0:ATT].bitcast(F16).rearrange("p (q s w) -> p q s w", q=PIECES, s=2)

        class Layout:

            def __init__(self, at=0):
                self.at = at

            def __call__(self, shape, dt=F32, rows=P):
                n = int(np.prod(shape))
                words = n if dt != F16 else (n + 1) // 2
                v = space[0:rows, ATT + self.at:ATT + self.at + words]
                self.at += words
                assert self.at <= ARENA, self.at
                if dt != F32:
                    v = v.bitcast(dt)
                if len(shape) > 1:
                    names = " ".join("abcd"[:len(shape)])
                    v = v.rearrange(f"p ({names}) -> p {names}", **dict(zip("abcd", shape)))
                return v

        WEND = E * FW - ATT
        wflat = [Layout(0)([E * 2 * FW], F16), Layout(-ATT)([E * 2 * FW], F16)]
        wexp, wexp2 = (w.rearrange("p (e w) -> p e w", e=E) for w in wflat)
        lay = Layout(E * FW)
        b1_bc = lay([E * HID])
        moe_at = lay.at
        xg = lay([2, D])
        xh, xl = lay([2, D], F16), lay([2, D], F16)
        z = lay([2, HID])
        hact = lay([2, KH * P])
        hh, hl = lay([2, KH, P], F16), lay([2, KH, P], F16)
        yo = lay([2, D])
        late_at = lay.at
        lay = Layout(moe_at)
        lg_first = lay([NCH, TPC, D])
        xnT_first = lay([2, KD, P])
        lay2 = Layout(STAGES * FW - ATT)
        late = Layout(late_at)
        OHlo, OHhi = [], []
        for at in (lay2, late):
            OHlo.append(at([2, NT, P], F16))
            OHhi.append(at([2, NT, SLOT_TILES + 1], F16))
        assert lay2.at <= 0
        apiece = Layout(late_at)([PIECE])
        lay = Layout(max(late.at, lay.at))
        S, S2, OH1, OH2, KEY, M8, QP = (lay([NT, E]) for _ in range(7))
        CE, SC, EX = (lay([E, NT]) for _ in range(3))
        m1, m2, k1, dm, th = (lay([NT]) for _ in range(5))
        posf, hi_f, lo_f = (lay([2, NT]) for _ in range(3))
        hi16, lo16 = (lay([2, NT], F16) for _ in range(2))
        tl, en, st8, base8, one8 = (lay([E]) for _ in range(5))
        cmp = lay([SLOT_TILES, E])
        evf = lay([SLOT_TILES])
        wstage = Layout(-ATT)([STAGES, FW])

        lay = Layout()
        raw = lay([PAIRS, 4, CH + HALO])
        xTh, xTl = lay([KD, CH], F16), lay([KD, CH], F16)
        abt, abs_ = lay([CH], rows=44), lay([CH], rows=44)
        sigab = lay([CH], F16, rows=44)
        carry = lay([PAIRS, 2])
        msq, root_ = lay([TPC, 2]), lay([TPC, 2])
        rootb = lay([TPC, 2, P // 2])
        assert lay.at <= WEND - 2 * D
        lay = Layout(WEND - 2 * D)
        xnt = lay([2, D])
        yg = lay([TPC, 2, D])
        xgrp = lay([TPC, D])
        sg = lay([PAIRS, 2, CH])
        ang, rnd, frac, sn, af, cs = (lay([CH]) for _ in range(6))
        vcon = lay([2, CH])
        tmp = lay([4, CH])
        res = lay([PAIRS, 2, CH])
        sqs = lay([2, CH])
        sqa = lay([CH])
        on = lay([2, CH])
        oh, ol = lay([2 * PAIRS, CH], F16), lay([2 * PAIRS, CH], F16)
        ob = lay([2, D])
        x1t = lay([2, D])
        x2t = lay([2, D])
        lay = Layout(WEND)
        lg = [lg_first, lay([NCH, TPC, D])]
        xnT = [xnT_first, Layout(WEND - 2 * D)([2, KD, P])]
        x2_tail = lay([TPC, D])
        rows_last = [lg[1][:, g] for g in range(NCH - 1)] + [x2_tail]
        yg_last = lay([NT, 2, D])

        bank = [ctx.enter_context(nc.psum_tensor(f"bank{i}", [P, 512], F32)) for i in range(8)]

        def w1(ph, part, k, ev):
            return wflat[ph][:, bass.ds(ev * (2 * FW) + (part * FW + k * HID), HID)]

        def w2(ph, part, c, ev):
            return wflat[ph][:, bass.ds(ev * (2 * FW) + (part * FW + KD * HID + c * D), D)]

        def w_proj(part, k, col):
            at = k * NCOL + col
            return att[:, at // BLOCK, part, at % BLOCK:at % BLOCK + P]

        def w_ab(part, k):
            return att[:, k, part, BLOCK:PIECE]

        def w_out(part, r):
            at = KD * NCOL + r * D
            return att[:, at // BLOCK, part, at % BLOCK:at % BLOCK + D]

        consts = sem("consts")
        params = sem("params")
        b1_in = [sem("b1_in"), sem("b1_back")]
        w_in = [sem(f"w_in{i}") for i in range(STAGES)]
        w_hi = sem("w_hi")
        w_ready = sem("w_ready")
        w_save = sem("w_save")
        w_back = sem("w_back")
        a_in = sem("a_in")
        a_hi, a_lo = sem("a_hi"), sem("a_lo")
        g_in = [sem(f"g_in{i}") for i in range(NCH)]
        s_rstd = sem("s_rstd")
        s_xn = sem("s_xn")
        g_out = [sem(f"g_out{i}") for i in range(NCH)]
        s_xt = sem("s_xt")
        s_xtc = sem("s_xtc")
        s_gate = sem("s_gate")
        s_onehot = sem("s_onehot")
        s_dm = sem("s_dm")
        s_tanh = sem("s_tanh")
        s_count = sem("s_count")
        s_ohs = sem("s_ohs")
        s_inv = sem("s_inv")
        s_route = sem("s_route")
        xg_in = [sem("xg_in0"), sem("xg_in1")]
        m_xt, m_z, m_ht, m_y = (sem(n) for n in ("m_xt", "m_z", "m_ht", "m_y"))
        m_xh, m_h, m_hh = (sem(n) for n in ("m_xh", "m_h", "m_hh"))
        m_xl, m_zb, m_hl, m_yo = (sem(n) for n in ("m_xl", "m_zb", "m_hl", "m_yo"))
        m_yst = [sem("m_yst0"), sem("m_yst1")]
        dve = sem("dve")
        pool = sem("pool")
        actc = sem("actc")
        cg_in = sem("cg_in")
        yg_in = [sem(f"yg_in{i}") for i in range(4)]
        yl_in = [sem(f"yl_in{i}") for i in range(NT)]
        c_comb = sem("c_comb")
        x1_st = sem("x1_st")
        c_rstd, c_xn, c_xt, c_xh, c_xl = (sem(n) for n in ("c_rstd", "c_xn", "c_xt", "c_xh", "c_xl"))
        c_ab, c_th, c_sig, c_sgh, c_sgl = (sem(n) for n in ("c_ab", "c_th", "c_sig", "c_sgh", "c_sgl"))
        c_proj, c_ev, c_frac, c_trig, c_conv = (sem(n) for n in ("c_proj", "c_ev", "c_frac", "c_trig", "c_conv"))
        c_bc, c_scan, c_sq, c_sqa, c_ssq = (sem(n) for n in ("c_bc", "c_scan", "c_sq", "c_sqa", "c_ssq"))
        c_ms, c_pow, c_rb, c_root = (sem(n) for n in ("c_ms", "c_pow", "c_rb", "c_root"))
        c_norm, c_out, c_ob, c_x2 = (sem(n) for n in ("c_norm", "c_out", "c_ob", "c_x2"))
        dve_on = sem("dve_on")
        c_on, c_gated, c_oh = (sem(n) for n in ("c_on", "c_gated", "c_oh"))
        x1t_in = [sem("x1t_in0"), sem("x1t_in1")]
        x2_st = [sem("x2_st0"), sem("x2_st1")]
        f_out, f_comb = sem("f_out"), sem("f_comb")
        zero_init = sem("zero_init")

        block = ctx.enter_context(nc.Block())

        def rows4(ap, g):
            return ap[bass.ds(g * CH, CH), :].rearrange("(a p) d -> p a d", p=P)

        @block.sync
        def _(sp):
            for dst, src in ((gw[:, :, :], gate_wT.rearrange("(k p) e -> p k e", p=P)),
                             (gb[:, :, :], gate_bias.partition_broadcast(P)),
                             (conv_sb[:, :, :, :], conv), (rms_sb[:, :], rms_w), (turns_sb[:, :], turns)):
                sp.dma_start(dst, src).then_inc(params, 16)
            for par in (0, 1):
                sp.sem_inc(m_yst[par], 1)
                sp.sem_inc(x2_st[par], 1)

            def fetch_group(ph, g):
                sp.dma_start(lg[ph][:, g], rows4(x2_rows if ph else x_in, g)).then_inc(g_in[g], 16)

            def store_group(ph, g):
                sp.wait_ge(s_xn, NT * ph + TPC * (g + 1))
                sp.dma_start(rows4(xn_rows, g), lg[ph][:, g]).then_inc(g_out[g], 16)

            def slots(ph):
                def store(t, par):
                    sp.wait_ge(m_yo, SLOT_TILES * ph + t + 3)
                    sp.dma_start(slot_out[bass.ds(t * P, P), :], yo[:, par]).then_inc(m_yst[par], 16)

                def turn(j, pieces, keep=False):
                    if keep:
                        sp.dma_start(w_saved[bass.ds(j, 1), :, :].rearrange("a p w -> p (a w)"),
                                     wexp[:, bass.ds(j, 1), :].rearrange("p a w -> p (a w)")).then_inc(w_save, 16)
                    if pieces:
                        sp.wait_ge(a_lo, j + 1)
                        sp.dma_start(apiece, att_w[bass.ds(j, 1), :, :].rearrange("a p w -> p (a w)")).then_inc(a_in, 16)
                    store(2 * j, 0)
                    store(2 * j + 1, 1)

                split = 0 if ph else PIECES
                if split:
                    sp.wait_ge(s_inv, 1)
                    sp.wait_ge(w_ready, E)
                    for g in range(NCH):
                        sp.wait_ge(g_out[g], 16)
                    with sp.Fori(0, E) as j:
                        turn(j, True, True)
                    with sp.Fori(E, split) as j:
                        turn(j, True)
                with sp.Fori(split, SLOT_TILES // 2) as j:
                    turn(j, False)
                store(SLOT_TILES - 1, 0)

            def outputs_stored(ph):
                for par in (0, 1):
                    sp.wait_ge(m_yst[par], 16 * (ph + 1) * (SLOT_TILES // 2 + 1 - par) + 1)

            for g in range(NCH):
                fetch_group(0, g)
            for g in range(NCH):
                store_group(0, g)
            slots(0)
            outputs_stored(0)

            def group_in(c):
                sp.dma_start(xgrp, rows4(x_in, c)).then_inc(cg_in, 16)

            def group_out(c):
                sp.wait_ge(c_comb, TPC * (c + 1))
                sp.dma_start(rows4(x1_rows, c), xgrp).then_inc(x1_st, 16)

            def next_group_in(c):
                sp.wait_ge(x1_st, 16 * c)
                sp.wait_ge(c_xn, TPC * c)
                group_in(c)

            def x1_in(c, i):
                n = TPC * c + i
                sp.wait_ge(c_x2, n + 1)
                sp.dma_start(x1t[:, i % 2], x1_rows[bass.ds(n * P, P), :]).then_inc(x1t_in[i % 2], 16)

            def out_tiles(c):
                for i in range(TPC):
                    n = TPC * c + i
                    sp.wait_ge(c_x2, n + 3)
                    sp.dma_start(x2_rows[bass.ds(n * P, P), :], x2t[:, i % 2]).then_inc(x2_st[i % 2], 16)
                    if i + 2 < TPC:
                        x1_in(c, i + 2)

            def x2_stored(chunks):
                for par in (0, 1):
                    sp.wait_ge(x2_st[par], 16 * (TPC // 2) * chunks + 1)

            def expert_back(e):
                sp.dma_start(wexp2[:, e], w_saved[e, :, :]).then_inc(w_back, 16)

            sp.wait_ge(w_save, 16 * E)
            group_in(0)
            group_out(0)
            next_group_in(1)
            group_out(1)
            for c in range(1, NCH - 1):
                next_group_in(c + 1)
                for i in (0, 1):
                    x1_in(c - 1, i)
                out_tiles(c - 1)
                group_out(c + 1)
            for i in (0, 1):
                x1_in(NCH - 2, i)
            sp.wait_ge(x1_st, 16 * NCH)
            sp.wait_ge(c_xn, TPC * NCH)
            x2_stored(NCH - 2)
            for g in range(NCH - 2):
                fetch_group(1, g)
            out_tiles(NCH - 2)
            for i in (0, 1):
                x1_in(NCH - 1, i)
            x2_stored(NCH - 1)
            fetch_group(1, NCH - 2)
            sp.wait_ge(c_proj, KINDS * PAIRS * NCH)
            sp.wait_ge(c_conv, PAIRS * NCH + 3)
            for e in (0, 1, 2, 5, 6):
                expert_back(e)
            for g in range(NCH - 1):
                store_group(1, g)
            for i in (2, 3):
                x1_in(NCH - 1, i)

            sp.wait_ge(c_out, NT + 1)
            for e in (3, 4):
                expert_back(e)
            sp.wait_ge(c_x2, NT + 2)
            sp.dma_start(b1_bc, b1.partition_broadcast(P)).then_inc(b1_in[1], 16)
            store_group(1, NCH - 1)
            sp.wait_ge(s_gate, 2 * NT + 2)
            expert_back(7)
            for g in range(NCH - 1):
                sp.wait_ge(g_out[g], 16 * 2)
                sp.dma_start(rows_last[g], rows4(x2_rows, g)).then_inc(g_in[g], 16)
            slots(1)
            outputs_stored(1)

            for g in range(NCH - 1):
                sp.wait_ge(f_comb, TPC * (g + 1))
                sp.dma_start(rows4(out, g), rows_last[g]).then_inc(f_out, 16)
            for n in range(NT - TPC, NT):
                sp.wait_ge(f_comb, n + 1)
                sp.dma_start(out[bass.ds(n * P, P), :], x2_tail[:, n % TPC]).then_inc(f_out, 16)
            sp.wait_ge(f_out, 16 * (NCH - 1 + TPC))

        @block.gpsimd
        def _(gp):
            ch = Chain(gp, pool)

            def seq(ins):
                ch(ins)
                ch.wait()

            def select(out_, in_, op, fill, base, pattern, per_row):
                seq(gp.affine_select(out=out_, in_=in_, compare_op=op, fill=fill, base=base, pattern=pattern,
                                     channel_multiplier=per_row))

            def count(out_, base, pattern, per_row):
                return gp.iota(out_, pattern=pattern, base=base, channel_multiplier=per_row,
                               allow_small_or_imprecise_dtypes=True)

            for buf, value in ((ident, 0.0), (ones, 1.0), (headmean, 1.0 / P), (sel, 0.0),
                               (half_pi, PI2 / 4), (epsc, EPS), (restart, 1.0), (power, -0.5)):
                seq(gp.memset(buf.ap(), value))
            seq(gp.memset(restart[:, :, 0:1], 0.0))
            seq(gp.memset(headmean[0:64, 64:128], 0.0))
            seq(gp.memset(headmean[64:128, 0:64], 0.0))
            select(ident[:, :], ident[:, :], ALU.not_equal, 1.0, 0, [[-1, P]], 1)
            select(before[:, :], ones[:, :], ALU.is_gt, 0.0, 0, [[1, P]], -1)
            sel_rows = sel[:, :, :, :].rearrange("r t p (h c) -> r (t p h) c", h=2)
            for first in (0, 32):
                select(sel_rows, sel_rows, ALU.not_equal, 1.0, -first, [[-1, NAB], [0, 64]], 1)
            seq(count(desc[:, :, :], E, [[0, NT], [-1, E]], 0))
            seq(count(lane[:, :], 0, [[1, P]], 0))
            count(tokid[:, :], 0, [[P, NT]], 1).then_inc(consts, 1)
            gp.wait_ge(consts, 1)
            gp.dma_start(b1_bc, b1.partition_broadcast(P)).then_inc(b1_in[0], 16)
            for e in range(E):
                if e < STAGES:
                    gp.wait_ge(g_in[e + 1], 16)
                else:
                    gp.wait_ge(w_ready, e - STAGES + 1)
                gp.dma_start(wstage[:, e % STAGES], ffn_w[e, :, :]).then_inc(w_in[e % STAGES], 16)

            def gather(dst, rows, index, done):
                gp.indirect_dma_start(dst, None, rows, bass.IndirectOffsetOnAxis(ap=index, axis=0)).then_inc(done, 16)

            def slots(ph):
                gp.wait_ge(s_route, ph + 1)
                for g in range(NCH):
                    gp.wait_ge(g_out[g], 16 * (ph + 1))
                for t in range(SLOT_TILES):
                    gp.wait_ge(m_xt, SLOT_TILES * ph + t + 1)
                    gather(xg[:, t % 2], xn_rows, slot_tok[:, t:t + 1], xg_in[t % 2])

            def fetch_outputs(c):
                for i in range(TPC):
                    n = TPC * c + i
                    if c:
                        gp.wait_ge(c_comb, n - TPC + 1)
                    for k in (0, 1):
                        gather(yg[:, i, k], slot_out, pos_i[:, k, n:n + 1], yg_in[i])

            def root_of(u):
                gp.wait_ge(c_ms, u + 1)
                gp.tensor_tensor(root_, msq, power[:, :, :], ALU.pow).then_inc(c_pow, 1)

            def add_squares(u):
                gp.wait_ge(c_sq, u + 1)
                gp.wait_ge(c_ssq, u + 1)
                gp.tensor_tensor(sqa, sqs[:, 0], sqs[:, 1], ALU.add).then_inc(c_sqa, 1)

            def apply_gate(u, p):
                gp.wait_ge(c_on, u + 2)
                for eo in (0, 1):
                    last = gp.tensor_tensor(on[:, eo], on[:, eo], sg[:, p, eo], ALU.mult)
                last.then_inc(c_gated, 1)

            def add_out(c, keep=False):
                for i in range(TPC):
                    n, j = TPC * c + i, 2 * c + i // 2
                    gp.wait_ge(c_ob, n + 3)
                    gp.wait_ge(x1t_in[i % 2], 16 * (j + 1))
                    if keep:
                        dst = x2_tail[:, i]
                    else:
                        gp.wait_ge(x2_st[i % 2], 16 * j + 1)
                        dst = x2t[:, i % 2]
                    gp.tensor_tensor(dst, ob[:, i % 2], x1t[:, i % 2], ALU.add).then_inc(c_x2, 1)

            def outputs_stored(ph):
                for par in (0, 1):
                    gp.wait_ge(m_yst[par], 16 * (ph + 1) * (SLOT_TILES // 2 + 1 - par) + 1)

            gp.sem_inc(c_x2, 2)
            gp.sem_inc(c_sqa, 1)
            slots(0)
            outputs_stored(0)
            gp.wait_ge(w_save, 16 * E)
            fetch_outputs(0)
            for c in range(NCH):
                if c:
                    apply_gate(3 * c - 2, 1)
                    root_of(3 * c - 1)
                if c < NCH - 1:
                    fetch_outputs(c + 1)
                if c:
                    apply_gate(3 * c - 1, 2)
                add_squares(3 * c)
                root_of(3 * c)
                if c:
                    add_out(c - 1)
                add_squares(3 * c + 1)
                apply_gate(3 * c, 0)
                root_of(3 * c + 1)
                add_squares(3 * c + 2)
            root_of(3 * NCH - 1)
            add_out(NCH - 1, True)
            slots(1)
            outputs_stored(1)
            for n in range(NT):
                for k in (0, 1):
                    gather(yg_last[:, n, k], slot_out, pos_i[:, k, n:n + 1], yl_in[n])

        @block.tensor
        def _(pe):
            def transpose4(dst, src):
                for k in range(KD):
                    last = pe.transpose(dst[:, k * P:(k + 1) * P], src[:, k * P:(k + 1) * P], ident[:, :])
                return last

            def products(dst, terms):
                for n, (a, b) in enumerate(terms):
                    last = pe.matmul(dst, a, b, start=(n == 0), stop=(n == len(terms) - 1))
                return last

            def score_group(ph, g):
                o = NT * ph

                def xt(n):
                    pe.wait_ge(s_xn, o + n + 1)
                    pe.wait_ge(s_xtc, o + n + 1)
                    transpose4(bank[n % 2], lg[ph][:, n // TPC, n % TPC]).then_inc(s_xt, 1)

                def score(n):
                    pe.wait_ge(s_xtc, o + n + 3)
                    products(bank[2][:, n * E:(n + 1) * E],
                             [(xnT[ph][:, n % 2, k, :], gw[:, k, :]) for k in range(KD)]).then_inc(s_gate, 1)

                xt(TPC * g)
                for n in range(TPC * g + 1, TPC * (g + 1)):
                    xt(n)
                    score(n - 1)
                score(TPC * (g + 1) - 1)

            def route(ph):
                pe.wait_ge(s_onehot, ph + 1)
                chosen = M8.rearrange("p a b -> p (a b)")
                products(bank[3][:, 0:NT * E], [(before[:, :], chosen)])
                products(bank[4][:, 0:NT * E], [(ones[:, :], chosen)]).then_inc(s_count, 1)
                pe.wait_ge(s_ohs, ph + 1)
                products(bank[5][:, 0:SLOT_TILES],
                         [(OHlo[ph][:, k, t, :], OHhi[ph][:, k, t, 0:SLOT_TILES]) for k in (0, 1) for t in range(NT)]).then_inc(s_inv, 1)

            def slots(ph):
                o = SLOT_TILES * ph
                g = (SLOT_TILES // 2 + 1) * ph

                def xt(t, j, par):
                    pe.wait_ge(xg_in[par], 16 * (g - par * ph + j + 1))
                    pe.wait_ge(m_xl, o + t + 1)
                    transpose4(bank[par], xg[:, par]).then_inc(m_xt, 1)

                def up(t, par):
                    ev = pe.value_load(tile_exp[0:1, bass.ds(t, 1)], min_val=0, max_val=E - 1)
                    pe.wait_ge(m_xl, o + t + 3)
                    pe.wait_ge(m_zb, o + t + 1)
                    products(bank[2 + par][:, 0:HID],
                             [(a[:, par, k * P:(k + 1) * P], w1(ph, part, k, ev))
                              for k in range(KD) for a, part in ((xh, 0), (xh, 1), (xl, 0))]).then_inc(m_z, 1)
                    return ev

                def ht(t, par):
                    pe.wait_ge(m_h, o + t + 3)
                    pe.wait_ge(m_hl, o + t + 1)
                    for c in range(KH):
                        last = pe.transpose(bank[4 + par][:, c * P:(c + 1) * P], hact[:, par, c * P:(c + 1) * P], ident[:, :])
                    last.then_inc(m_ht, 1)

                def down(t, par):
                    ev = pe.value_load(tile_exp[0:1, bass.ds(t, 1)], min_val=0, max_val=E - 1)
                    pe.wait_ge(m_hl, o + t + 3)
                    pe.wait_ge(m_yo, o + t + 1)
                    products(bank[6 + par][:, :],
                             [(a[:, par, c, :], w2(ph, part, c, ev)) for c in range(KH)
                              for a, part in ((hh, 0), (hh, 1), (hl, 0))]).then_inc(m_y, 1)

                pe.wait_ge(s_route, ph + 1)
                xt(0, 0, 0)
                if ph == 0:
                    pe.wait_ge(w_ready, E)
                else:
                    pe.wait_ge(w_back, 16 * E)
                up(0, 0)
                xt(1, 0, 1)

                def step(t, j, par):
                    other = 1 - par
                    ht(t, par)
                    up(t + 1, other)
                    xt(t + 2, j + 1, par)
                    down(t, par)

                with pe.Fori(0, SLOT_TILES // 2 - 1) as j:
                    step(2 * j, j, 0)
                    step(2 * j + 1, j, 1)
                t = SLOT_TILES - 3
                step(t, t // 2, 0)
                ht(t + 1, 1)
                up(t + 2, 0)
                down(t + 1, 1)
                ht(t + 2, 0)
                down(t + 2, 0)

            def transpose_rows(c, tiles):
                for i in tiles:
                    pe.wait_ge(c_xn, TPC * c + i + 1)
                    if i < 3:
                        pe.wait_ge(c_ev, KINDS * PAIRS * c + i + 1)
                    else:
                        pe.wait_ge(c_xl, TPC * c + i - 2)
                    transpose4(bank[i % 3], xnt[:, i % 2]).then_inc(c_xt, 1)

            def logits(c):
                pe.wait_ge(c_xl, TPC * (c + 1))
                products(bank[6][0:NAB, :],
                         [(w_ab(part, k), x[:, k, :])
                          for k in range(KD) for part, x in ((0, xTh), (1, xTh), (0, xTl))]).then_inc(c_ab, 1)

            def project(c, p, between={}):
                for kind in range(KINDS):
                    if kind in between:
                        between[kind]()
                    m = KINDS * (PAIRS * c + p) + kind
                    col = (p * KINDS + kind) * P
                    pe.wait_ge(c_ev, m + 1)
                    products(bank[kind % 3][:, :],
                             [(w_proj(part, k, col), x[:, k, :])
                              for k in range(KD) for part, x in ((0, xTh), (1, xTh), (0, xTl))]).then_inc(c_proj, 1)

            def spread(c, p):
                pe.wait_ge(c_sgl, c + 1)
                pe.wait_ge(c_scan, PAIRS * c + p + 1)
                products(bank[3][:, :], [(sel[:, 1, p, :], sigab)])
                products(bank[4][:, :], [(sel[:, 0, p, :], sigab)]).then_inc(c_bc, 1)

            def mean_square(u):
                pe.wait_ge(c_sqa, u + 2)
                for i in range(TPC):
                    last = products(bank[7][:, 2 * i:2 * i + 2], [(sqa[:, i * P:(i + 1) * P], heads)])
                last.then_inc(c_ssq, 1)

            def spread_roots(u):
                pe.wait_ge(c_rb, u + 1)
                pe.wait_ge(c_on, u + 1)
                for i in range(TPC):
                    last = products(bank[5][:, i * P:(i + 1) * P],
                                    [(rootb[:, i].rearrange("p h c -> p (h c)"), ident[:, :])])
                last.then_inc(c_root, 1)

            def project_out(c, roots):
                pe.wait_ge(c_norm, PAIRS * (c + 1) + 3)
                pe.wait_ge(c_th, c + 1)
                for i in range(TPC):
                    pe.wait_ge(c_ob, TPC * c + i + 1)
                    if i == 1 and roots is not None:
                        spread_roots(roots)
                    products(bank[6 + i % 2][:, :],
                             [(a[:, r, i * P:(i + 1) * P], w_out(part, r))
                              for r in range(2 * PAIRS) for a, part in ((oh, 0), (oh, 1), (ol, 0))]).then_inc(c_out, 1)

            def project_last(c):
                def part(i, units, start, stop):
                    terms = [(a[:, r, i * P:(i + 1) * P], w_out(w, r)) for r in units for a, w in ((oh, 0), (oh, 1), (ol, 0))]
                    for n, (a, b) in enumerate(terms):
                        last = pe.matmul(bank[LAST_BANKS[i]][:, :], a, b, start=start and n == 0, stop=stop and n == len(terms) - 1)
                    return last

                pe.wait_ge(c_norm, PAIRS * (c + 1) + 2)
                pe.wait_ge(c_scan, PAIRS * (c + 1) + 1)
                pe.wait_ge(c_ob, TPC * c + 2)
                for i in range(TPC):
                    if i == 2:
                        spread_roots(3 * c + 2)
                    part(i, range(4), True, False)
                pe.wait_ge(c_norm, PAIRS * (c + 1) + 3)
                for i in range(TPC):
                    part(i, (4, 5), False, True).then_inc(c_out, 1)

            def chunk(c, first, last):
                def unit_1_squares():
                    if not first:
                        pe.wait_ge(c_ob, TPC * c + 2)
                    mean_square(3 * c + 1)

                u = 3 * c
                project(c, 0, {} if first else {4: lambda: mean_square(u - 1)})
                spread(c, 0)
                project(c, 1, {} if first else {1: lambda: spread_roots(u - 1)})
                spread(c, 1)
                mean_square(u)
                if first:
                    spread_roots(u)
                else:
                    project_out(c - 1, u)
                project(c, 2, {2: unit_1_squares, 5: lambda: spread_roots(u + 1)})
                if last:
                    spread(c, 2)
                else:
                    transpose_rows(c + 1, (0, 1))
                    spread(c, 2)
                    transpose_rows(c + 1, (2, 3))
                    logits(c + 1)

            heads = headmean[:, :].rearrange("p (h c) -> p h c", h=2)[:, :, 0]
            for s, n in ((s_gate, 2), (m_xt, 2), (m_z, 2), (m_ht, 2), (m_y, 2), (c_xt, 2), (c_ssq, 1), (c_out, 1), (c_root, 1)):
                pe.sem_inc(s, n)
            pe.wait_ge(consts, 1)
            pe.wait_ge(params, 16 * 5)
            for g in range(NCH):
                score_group(0, g)
            route(0)
            slots(0)
            pe.wait_ge(a_lo, PIECES + 1)
            transpose_rows(0, range(TPC))
            logits(0)
            chunk(0, True, False)
            with pe.Fori(1, NCH - 1) as c:
                chunk(c, False, False)
            chunk(NCH - 1, False, True)
            pe.wait_ge(c_ev, KINDS * PAIRS * NCH + 3)
            score_group(1, 0)
            mean_square(3 * NCH - 1)
            project_last(NCH - 1)
            score_group(1, 1)
            score_group(1, 2)
            score_group(1, 3)
            route(1)
            slots(1)

        @block.scalar
        def _(act):
            ch = Chain(act, actc)

            def split_high(e):
                act.wait_ge(w_in[e % STAGES], 16 * (e // STAGES + 1))
                act.activation(wexp[:, e, 0:FW], wstage[:, e % STAGES], ACT.Copy, scale=WSCALE).then_inc(w_hi, 1)

            def normalise_group(ph, g):
                normalise_rows(ph, g, lg[ph][:, g])
                copy_transposed(ph, g)

            def normalise_rows(ph, g, rows):
                act.wait_ge(s_rstd, NCH * ph + g + 1)
                for i in range(TPC):
                    act.activation(lg[ph][:, g, i], rows[:, i], ACT.Identity, scale=rstd[:, g, 0, i:i + 1],
                                   bias=rstd[:, g, 1, i:i + 1]).then_inc(s_xn, 1)

            def copy_transposed(ph, g):
                o = NT * ph
                for n in range(TPC * g, TPC * (g + 1)):
                    act.wait_ge(s_xt, o + n + 1)
                    act.wait_ge(s_gate, o + n + 1)
                    act.activation(xnT[ph][:, n % 2].rearrange("p k c -> p (k c)"), bank[n % 2][:, :], ACT.Copy).then_inc(s_xtc, 1)

            def slots(ph):
                o = SLOT_TILES * ph

                def x_high(t, par):
                    act.wait_ge(m_xt, o + t + 3)
                    act.wait_ge(m_z, o + t + 1)
                    act.activation(xh[:, par], bank[par][:, :], ACT.Copy).then_inc(m_xh, 1)

                def silu(t, par):
                    act.wait_ge(m_zb, o + t + 3)
                    act.wait_ge(m_ht, o + t + 1)
                    act.activation(hact[:, par, 0:HID], z[:, par], ACT.Silu).then_inc(m_h, 1)

                def h_high(t, par):
                    act.wait_ge(m_ht, o + t + 3)
                    act.wait_ge(m_y, o + t + 1)
                    act.activation(hh[:, par].rearrange("p a b -> p (a b)"), bank[4 + par][:, 0:KH * P], ACT.Copy).then_inc(m_hh, 1)

                def piece(q):
                    act.wait_ge(a_in, 16 * (q + 1))
                    act.activation(att[:, bass.ds(q, 1), 0, :].rearrange("p a w -> p (a w)"), apiece, ACT.Copy, scale=WSCALE).then_inc(a_hi, 1)

                def step(t, par):
                    h_high(t, par)
                    silu(t + 1, 1 - par)
                    x_high(t + 2, par)

                x_high(0, 0)
                silu(0, 0)
                x_high(1, 1)
                split = 0 if ph else PIECES
                if split:
                    with act.Fori(0, split) as j:
                        step(2 * j, 0)
                        step(2 * j + 1, 1)
                        piece(j)
                with act.Fori(split, SLOT_TILES // 2 - 1) as j:
                    step(2 * j, 0)
                    step(2 * j + 1, 1)
                t = SLOT_TILES - 3
                step(t, 0)
                h_high(t + 1, 1)
                silu(t + 2, 0)
                h_high(t + 2, 0)

            def normalise(c, i):
                act.wait_ge(c_rstd, c + 1)
                act.wait_ge(c_xt, TPC * c + i + 1)
                act.activation(xnt[:, i % 2], xgrp[:, i], ACT.Identity, scale=rstd[:, 0, 0, i:i + 1],
                               bias=rstd[:, 0, 1, i:i + 1]).then_inc(c_xn, 1)

            def x_high(c, i):
                act.wait_ge(c_xt, TPC * c + i + 3)
                act.activation(xTh[:, :, i * P:(i + 1) * P], bank[i % 3][:, :].rearrange("p (k c) -> p k c", k=KD),
                               ACT.Copy).then_inc(c_xh, 1)

            def logits_tanh(c):
                act.wait_ge(c_ab, c + 1)
                act.activation(abt[0:NAB], bank[6][0:NAB, :], ACT.Tanh, scale=0.5 * UNSCALE).then_inc(c_th, 1)

            def sigmoid_high(c):
                act.wait_ge(c_sig, c + 1)
                if not (isinstance(c, int) and c == 0):
                    act.wait_ge(c_bc, PAIRS * c)
                act.activation(sigab[0:NAB], abs_[0:NAB], ACT.Copy).then_inc(c_sgh, 1)

            def evacuate(c, p, kinds):
                u = PAIRS * c + p
                for kind in kinds:
                    act.wait_ge(c_proj, KINDS * u + kind + 1)
                    if kind < 4:
                        act.wait_ge(c_conv, u + 1)
                        act.activation(raw[:, p, kind, HALO:], bank[kind % 3][:, :], ACT.Copy, scale=UNSCALE).then_inc(c_ev, 1)
                    else:
                        act.wait_ge(c_norm, u + 1)
                        act.activation(sg[:, p, kind - 4], bank[kind % 3][:, :], ACT.Silu, scale=UNSCALE).then_inc(c_ev, 1)

            def trig(u):
                act.wait_ge(c_frac, u + 1)
                act.activation(sn, frac, ACT.Sin, scale=PI2)
                ch(act.activation(af, frac, ACT.Abs))
                ch.wait()
                act.activation(cs, af, ACT.Sin, scale=-PI2, bias=half_pi[:, 0:1]).then_inc(c_trig, 1)

            def mean_squares(u):
                act.wait_ge(c_ssq, u + 2)
                act.activation(msq.rearrange("p a b -> p (a b)"), bank[7][:, 0:2 * TPC], ACT.Identity,
                               bias=epsc[:, 0:1]).then_inc(c_ms, 1)

            def repeat_roots(u):
                act.wait_ge(c_pow, u + 1)
                act.wait_ge(c_root, u + 1)
                act.activation(rootb, root_.unsqueeze(3).to_broadcast([P, TPC, 2, P // 2]), ACT.Copy).then_inc(c_rb, 1)

            def gate_high(c, p):
                act.wait_ge(c_gated, PAIRS * c + p + 1)
                act.wait_ge(c_out, TPC * c + 1)
                for eo in (0, 1):
                    last = act.activation(oh[:, 2 * p + eo], on[:, eo], ACT.Copy)
                last.then_inc(c_oh, 1)

            def squares(u, p):
                act.wait_ge(c_scan, u + 2)
                act.wait_ge(c_sqa, u + 1)
                for eo in (0, 1):
                    last = act.activation(sqs[:, eo], res[:, p, eo], ACT.Square)
                last.then_inc(c_sq, 1)

            def chunk(c, first, last):
                u = 3 * c
                trig(u)
                evacuate(c, 1, range(5))
                squares(u, 0)
                evacuate(c, 1, (5,))
                if not first:
                    gate_high(c - 1, 2)
                trig(u + 1)
                mean_squares(u)
                repeat_roots(u)
                if not first:
                    out_tiles(c - 1)
                squares(u + 1, 1)
                if not last:
                    normalise(c + 1, 0)
                    normalise(c + 1, 1)
                evacuate(c, 2, (0, 1, 2))
                gate_high(c, 0)
                mean_squares(u + 1)
                evacuate(c, 2, (3,))
                repeat_roots(u + 1)
                evacuate(c, 2, (4, 5))
                if last:
                    trig(u + 2)
                    normalise_group(1, 0)
                    squares(u + 2, 2)
                else:
                    x_high(c + 1, 0)
                    normalise(c + 1, 2)
                    x_high(c + 1, 1)
                    normalise(c + 1, 3)
                    trig(u + 2)
                    x_high(c + 1, 2)
                    x_high(c + 1, 3)
                    logits_tanh(c + 1)
                    evacuate(c + 1, 0, (0, 1))
                    squares(u + 2, 2)
                    sigmoid_high(c + 1)
                    evacuate(c + 1, 0, (2, 3))
                    gate_high(c, 1)
                    evacuate(c + 1, 0, (4,))
                    mean_squares(u + 2)
                    evacuate(c + 1, 0, (5,))
                    repeat_roots(u + 2)

            def out_tiles(c, banks=(6, 7, 6, 7)):
                for i in range(TPC):
                    n = TPC * c + i
                    act.wait_ge(c_out, n + 2)
                    act.wait_ge(c_x2, n + 1)
                    act.activation(ob[:, i % 2], bank[banks[i]][:, :], ACT.Copy, scale=UNSCALE).then_inc(c_ob, 1)

            for s, n in ((s_xtc, 2), (m_h, 2), (c_ev, 3), (c_ob, 2)):
                act.sem_inc(s, n)
            act.wait_ge(consts, 1)
            for g in range(NCH):
                normalise_group(0, g)
            split_high(OWN)
            split_high(OWN + 1)
            act.wait_ge(s_dm, 1)
            act.activation(th, dm, ACT.Tanh, scale=0.5).then_inc(s_tanh, 1)
            for e in range(OWN + 2, E):
                split_high(e)
            slots(0)
            for i in (0, 1):
                normalise(0, i)
            for i in range(TPC):
                x_high(0, i)
                if i + 2 < TPC:
                    normalise(0, i + 2)
            logits_tanh(0)
            sigmoid_high(0)
            evacuate(0, 0, range(KINDS))
            chunk(0, True, False)
            ch.loop(1, NCH - 1, 3, lambda c: chunk(c, False, False))
            chunk(NCH - 1, False, True)
            mean_squares(3 * NCH - 1)
            normalise_rows(1, 1, lg[1][:, 1])
            repeat_roots(3 * NCH - 1)
            normalise_rows(1, 2, lg[1][:, 2])
            out_tiles(NCH - 1, LAST_BANKS)
            copy_transposed(1, 1)
            copy_transposed(1, 2)
            normalise_rows(1, 3, x2_tail)
            copy_transposed(1, 3)
            act.wait_ge(s_dm, 2)
            act.activation(th, dm, ACT.Tanh, scale=0.5).then_inc(s_tanh, 1)
            slots(1)

        @block.vector
        def _(v):
            ch = Chain(v, dve)

            def seq(ins):
                ch(ins)
                ch.wait()

            def inv_std(par, done):
                a, y, t1 = nt4[:, 0], nt4[:, 1], nt4[:, 2]
                ch(v.tensor_tensor(mv[:, :, 0], bst[:, :, 1], bst[:, :, 4], ALU.add))
                ch(v.tensor_tensor(mv[:, :, 1], bst[:, :, 1], bst[:, :, 4], ALU.subtract))
                seq(v.tensor_tensor(a, bst[:, :, 2], bst[:, :, 5], ALU.add))
                ch(v.scalar_tensor_tensor(t1, mv[:, :, 1], 0.25, mv[:, :, 1], ALU.mult, ALU.mult))
                seq(v.tensor_scalar(a, a, 1.0 / D, EPS, ALU.mult, ALU.add))
                seq(v.tensor_tensor(a, a, t1, ALU.add))
                seq(v.tensor_scalar(y.bitcast(I32), a.bitcast(I32), -0.5, RSQRT_SEED, ALU.mult, ALU.add))
                for _ in range(3):
                    seq(v.tensor_tensor(t1, y, y, ALU.mult))
                    seq(v.scalar_tensor_tensor(t1, t1, -0.5, a, ALU.mult, ALU.mult))
                    seq(v.scalar_tensor_tensor(y, t1, 1.5, y, ALU.add, ALU.mult))
                v.tensor_copy(rstd[:, par, 0], y)
                v.scalar_tensor_tensor(rstd[:, par, 1], mv[:, :, 0], -0.5, y, ALU.mult, ALU.mult).then_inc(done, 1)

            def stats(rows):
                for i in range(TPC):
                    ch(v.bn_stats(bst[:, i], rows[:, i]))
                ch.wait()

            def split_low(e):
                if e < OWN:
                    v.wait_ge(w_in[e % STAGES], 16 * (e // STAGES + 1))
                    seq(v.tensor_scalar(wexp[:, e, 0:FW], wstage[:, e % STAGES], WSCALE, None, ALU.mult))
                else:
                    v.wait_ge(w_hi, e - OWN + 1)
                v.scalar_tensor_tensor(wexp[:, e, FW:2 * FW], wstage[:, e % STAGES], WSCALE, wexp[:, e, 0:FW],
                                       ALU.mult, ALU.subtract).then_inc(w_ready, 1)

            def group_stats(ph, g, kept=False):
                if kept:
                    v.wait_ge(c_x2, NT + 2)
                    stats(x2_tail)
                else:
                    v.wait_ge(g_in[g], 16 * (ph + 1))
                    stats(lg[ph][:, g])
                inv_std(g, s_rstd)

            def round_down(dst, src, tmp_):
                seq(v.tensor_scalar(tmp_, src, -63.5, 1.0 / P, ALU.add, ALU.mult))
                seq(v.tensor_scalar(dst, tmp_, MAGIC, MAGIC, ALU.add, ALU.subtract))

            def route(ph):
                def bc(x):
                    return x.unsqueeze(2).to_broadcast([P, NT, E])

                def eb(x):
                    return x.unsqueeze(2).to_broadcast([P, E, NT])

                flat = "p a b -> p (a b)"
                v.wait_ge(s_gate, NT * (ph + 1) + 2)
                if ph == 0:
                    seq(v.tensor_tensor(gb[:, 0], gb[:, 0], gb[:, 1], ALU.add))
                seq(v.tensor_tensor(S, bank[2][:, 0:NT * E].rearrange("p (a b) -> p a b", b=E),
                                    gb[:, 0].unsqueeze(1).to_broadcast([P, NT, E]), ALU.add))
                seq(v.reduce_max(m1, S, AX))
                seq(v.tensor_tensor(KEY, S, bc(m1), ALU.is_equal))
                seq(v.tensor_tensor(KEY, KEY, desc[:, :, :], ALU.mult))
                seq(v.reduce_max(k1, KEY, AX))
                seq(v.tensor_tensor(OH1, desc[:, :, :], bc(k1), ALU.is_equal))
                seq(v.scalar_tensor_tensor(S2.rearrange(flat), OH1.rearrange(flat), 0.0, S.rearrange(flat), ALU.is_equal, ALU.mult))
                seq(v.scalar_tensor_tensor(S2.rearrange(flat), OH1.rearrange(flat), -3.0e38, S2.rearrange(flat), ALU.mult, ALU.add))
                seq(v.reduce_max(k1, S2, AX))
                v.tensor_tensor(dm, k1, m1, ALU.subtract).then_inc(s_dm, 1)
                seq(v.tensor_tensor(KEY, S2, bc(k1), ALU.is_equal))
                seq(v.tensor_tensor(KEY, KEY, desc[:, :, :], ALU.mult))
                seq(v.reduce_max(k1, KEY, AX))
                seq(v.tensor_tensor(OH2, desc[:, :, :], bc(k1), ALU.is_equal))
                v.tensor_tensor(M8, OH1, OH2, ALU.add).then_inc(s_onehot, 1)
                if ph == 0:
                    split_low(OWN)
                v.wait_ge(s_tanh, ph + 1)
                v.tensor_scalar(ghalf[:, 0], th, -0.25, 0.25, ALU.mult, ALU.add)
                v.tensor_scalar(ghalf[:, 1], th, 0.25, 0.25, ALU.mult, ALU.add)
                seq(v.memset(one8, 1.0))
                v.wait_ge(s_count, ph + 1)
                seq(v.tensor_copy(CE, bank[4][:, 0:NT * E].rearrange("p (t e) -> p e t", e=E)))
                seq(v.tensor_tensor_scan(SC.rearrange(flat), restart[:, :, :].rearrange(flat), CE.rearrange(flat), 0.0, ALU.mult, ALU.add))
                ch(v.tensor_tensor(EX, SC, CE, ALU.subtract))
                seq(v.tensor_scalar(tl, SC[:, :, NT - 1], float(P - 1), None, ALU.add))
                round_down(tl, tl, st8)
                seq(v.tensor_tensor_scan(en, one8, tl, 0.0, ALU.mult, ALU.add))
                seq(v.tensor_tensor(st8, en, tl, ALU.subtract))
                seq(v.tensor_scalar(base8, st8, float(P), None, ALU.mult))
                seq(v.tensor_tensor(EX, EX, eb(base8), ALU.add))
                seq(v.tensor_tensor(QP, bank[3][:, 0:NT * E].rearrange("p (a b) -> p a b", b=E),
                                    EX.rearrange("p e t -> p t e"), ALU.add))
                for k, oh_ in ((0, OH1), (1, OH2)):
                    seq(v.tensor_tensor(KEY, QP, oh_, ALU.mult))
                    seq(v.reduce_sum(posf[:, k], KEY, AX))
                ch(v.tensor_copy(pos_i[:, :, :], posf))
                round_down(hi_f, posf, lo_f)
                ch(v.tensor_copy(hi16, hi_f))
                seq(v.scalar_tensor_tensor(lo16, hi_f, -float(P), posf, ALU.mult, ALU.add))
                for k in (0, 1):
                    ch(v.tensor_tensor(OHlo[ph][:, k], lo16[:, k].unsqueeze(2).to_broadcast([P, NT, P]),
                                       lane16[:, :].unsqueeze(1).to_broadcast([P, NT, P]), ALU.is_equal))
                    seq(v.tensor_tensor(OHhi[ph][:, k, :, 0:SLOT_TILES], hi16[:, k].unsqueeze(2).to_broadcast([P, NT, SLOT_TILES]),
                                        lane16[:, 0:SLOT_TILES].unsqueeze(1).to_broadcast([P, NT, SLOT_TILES]), ALU.is_equal))
                    last = v.tensor_tensor(OHhi[ph][:, k, :, 0:SLOT_TILES], OHhi[ph][:, k, :, 0:SLOT_TILES],
                                           tokid16[:, :].unsqueeze(2).to_broadcast([P, NT, SLOT_TILES]), ALU.mult)
                    if k == 0:
                        ch(last)
                last.then_inc(s_ohs, 1)
                seq(v.tensor_tensor(cmp, lane[:, 0:SLOT_TILES].unsqueeze(2).to_broadcast([P, SLOT_TILES, E]),
                                    en.unsqueeze(1).to_broadcast([P, SLOT_TILES, E]), ALU.is_ge))
                seq(v.reduce_sum(evf, cmp, AX))
                seq(v.tensor_scalar(tile_exp[:, :], evf, float(E - 1), None, ALU.min))
                if ph == 0:
                    split_low(OWN + 1)
                v.wait_ge(s_inv, ph + 1)
                v.tensor_copy(slot_tok[:, :], bank[5][:, 0:SLOT_TILES]).then_inc(s_route, 1)
                if ph == 0:
                    for e in range(OWN + 2, E):
                        split_low(e)

            def slots(ph):
                o = SLOT_TILES * ph

                def x_low(t, par):
                    v.wait_ge(m_xh, o + t + 1)
                    v.tensor_tensor(xl[:, par], bank[par][:, :], xh[:, par], ALU.subtract).then_inc(m_xl, 1)

                def add_bias(t, par):
                    ev = v.value_load(tile_exp[0:1, bass.ds(t, 1)], min_val=0, max_val=E - 1)
                    v.wait_ge(m_z, o + t + 3)
                    v.wait_ge(m_h, o + t + 1)
                    v.scalar_tensor_tensor(z[:, par], bank[2 + par][:, 0:HID], UNSCALE, b1_bc[:, bass.ds(ev * HID, HID)],
                                           ALU.mult, ALU.add).then_inc(m_zb, 1)

                def h_low(t, par):
                    v.wait_ge(m_hh, o + t + 1)
                    v.tensor_tensor(hl[:, par].rearrange("p a b -> p (a b)"), bank[4 + par][:, 0:KH * P],
                                    hh[:, par].rearrange("p a b -> p (a b)"), ALU.subtract).then_inc(m_hl, 1)

                def y_out(t, j, par):
                    v.wait_ge(m_y, o + t + 3)
                    v.wait_ge(m_yst[par], 16 * ((SLOT_TILES // 2 + 1 - par) * ph + j) + 1)
                    v.tensor_scalar(yo[:, par], bank[6 + par][:, :], UNSCALE, None, ALU.mult).then_inc(m_yo, 1)

                def piece(q):
                    v.wait_ge(a_hi, q + 1)
                    v.scalar_tensor_tensor(att[:, bass.ds(q, 1), 1, :].rearrange("p a w -> p (a w)"), apiece, WSCALE,
                                           att[:, bass.ds(q, 1), 0, :].rearrange("p a w -> p (a w)"), ALU.mult, ALU.subtract).then_inc(a_lo, 1)

                def step(t, j, par):
                    h_low(t, par)
                    add_bias(t + 1, 1 - par)
                    x_low(t + 2, par)
                    y_out(t, j, par)

                for g in range(NCH):
                    v.wait_ge(g_out[g], 16 * (ph + 1))
                v.memset(hact[:, :, HID:HID + 1], 1.0)
                seq(v.memset(hact[:, :, HID + 1:KH * P], 0.0))
                v.wait_ge(b1_in[ph], 16)
                x_low(0, 0)
                add_bias(0, 0)
                x_low(1, 1)
                split = 0 if ph else PIECES
                if split:
                    with v.Fori(0, split) as j:
                        step(2 * j, j, 0)
                        step(2 * j + 1, j, 1)
                        piece(j)
                with v.Fori(split, SLOT_TILES // 2 - 1) as j:
                    step(2 * j, j, 0)
                    step(2 * j + 1, j, 1)
                t = SLOT_TILES - 3
                step(t, t // 2, 0)
                h_low(t + 1, 1)
                add_bias(t + 2, 0)
                y_out(t + 1, t // 2, 1)
                h_low(t + 2, 0)
                y_out(t + 2, t // 2 + 1, 0)

            def combine(g, rows, outputs, arrived, done):
                for i in range(TPC):
                    n = TPC * g + i
                    arrived(i)
                    seq(v.scalar_tensor_tensor(rows[:, i], outputs[:, i, 0], ghalf[:, 0, bass.ds(n, 1)], rows[:, i], ALU.mult, ALU.add))
                    v.scalar_tensor_tensor(rows[:, i], outputs[:, i, 1], ghalf[:, 1, bass.ds(n, 1)], rows[:, i], ALU.mult, ALU.add).then_inc(done, 1)

            def chunk_stats(c):
                v.wait_ge(cg_in, 16 * (c + 1))
                combine(c, xgrp, yg, lambda i: v.wait_ge(yg_in[i], 32 * (c + 1)), c_comb)
                v.wait_ge(c_comb, TPC * (c + 1))
                stats(xgrp)
                inv_std(0, c_rstd)

            def chunk_low(c):
                for i in range(TPC):
                    v.wait_ge(c_xh, TPC * c + i + 1)
                    v.tensor_tensor(xTl[:, :, i * P:(i + 1) * P], bank[i % 3][:, :].rearrange("p (k c) -> p k c", k=KD),
                                    xTh[:, :, i * P:(i + 1) * P], ALU.subtract).then_inc(c_xl, 1)

            def sigmoids(c):
                v.wait_ge(c_th, c + 1)
                v.tensor_scalar(abs_[0:NAB], abt[0:NAB], 0.5, 0.5, ALU.mult, ALU.add).then_inc(c_sig, 1)

            def sigmoids_low(c):
                v.wait_ge(c_sgh, c + 1)
                v.tensor_tensor(sigab[32:32 + NAB], abs_[0:NAB], sigab[0:NAB], ALU.subtract).then_inc(c_sgl, 1)

            def angles(c, p, between=lambda: None):
                u = PAIRS * c + p
                v.wait_ge(c_ev, KINDS * u + 2 + 3)
                seq(v.tensor_scalar(ang, raw[:, p, 0, 0:CH], cang[:, p, 0, 0:1], None, ALU.mult))
                for kind, j in [(0, 1), (0, 2), (0, 3), (1, 0), (1, 1), (1, 2), (1, 3)]:
                    seq(v.scalar_tensor_tensor(ang, raw[:, p, kind, j:j + CH], cang[:, p, kind, j:j + 1], ang, ALU.mult, ALU.add))
                seq(v.tensor_scalar(rnd, ang, MAGIC, MAGIC, ALU.add, ALU.subtract))
                v.tensor_tensor(frac, ang, rnd, ALU.subtract).then_inc(c_frac, 1)
                between()
                v.wait_ge(c_ev, KINDS * u + 4 + 3)
                for eo in (0, 1):
                    ch(v.tensor_scalar(vcon[:, eo], raw[:, p, 2 + eo, 0:CH], conv_sb[:, p, 2 + eo, 0:1], None, ALU.mult))
                for j in range(1, TAPS):
                    for eo in (0, 1):
                        ch.wait(ch.n - 1)
                        ch(v.scalar_tensor_tensor(vcon[:, eo], raw[:, p, 2 + eo, j:j + CH], conv_sb[:, p, 2 + eo, j:j + 1],
                                                  vcon[:, eo], ALU.mult, ALU.add))
                ch.wait()
                v.tensor_copy(raw[:, p, :, 0:HALO], raw[:, p, :, CH:CH + HALO]).then_inc(c_conv, 1)

            def recur(c, p):
                u = PAIRS * c + p
                v.wait_ge(c_trig, u + 1)
                v.wait_ge(c_bc, u + 1)
                ch(v.tensor_tensor(sn, bank[3][:, :], sn, ALU.mult))
                ch(v.tensor_tensor(cs, bank[3][:, :], cs, ALU.mult))
                ch.wait()
                ch(v.tensor_tensor(tmp[:, 0], vcon[:, 0], cs, ALU.mult))
                ch(v.tensor_tensor(tmp[:, 1], vcon[:, 1], sn, ALU.mult))
                ch(v.tensor_tensor(tmp[:, 2], vcon[:, 1], cs, ALU.mult))
                ch(v.tensor_tensor(tmp[:, 3], vcon[:, 0], sn, ALU.mult))
                ch.wait(ch.n - 2)
                ch(v.tensor_tensor(tmp[:, 0], tmp[:, 0], tmp[:, 1], ALU.subtract))
                ch.wait(ch.n - 1)
                ch(v.tensor_tensor(tmp[:, 2], tmp[:, 2], tmp[:, 3], ALU.add))
                ch.wait(ch.n - 1)
                v.tensor_tensor_scan(res[:, p, 0], bank[4][:, :], tmp[:, 0], carry[:, p, 0:1], ALU.mult, ALU.add)
                ch.wait()
                v.tensor_tensor_scan(res[:, p, 1], bank[4][:, :], tmp[:, 2], carry[:, p, 1:2], ALU.mult, ALU.add).then_inc(c_scan, 1)
                v.wait_ge(c_scan, u + 2)
                seq(v.tensor_copy(carry[:, p, :], res[:, p, :, CH - 1]))

            def gate(c, p):
                u = PAIRS * c + p
                v.wait_ge(c_root, u + 2)
                v.wait_ge(c_ev, KINDS * (u + 1) + 3)
                v.wait_ge(c_out, TPC * c + 1)
                for eo in (0, 1):
                    v.scalar_tensor_tensor(on[:, eo], res[:, p, eo], rms_sb[:, eo:eo + 1], bank[5][:, :],
                                           ALU.mult, ALU.mult).then_inc(c_on if eo else dve_on, 1)
                v.wait_ge(dve_on, u - (PAIRS * NCH - 3))
                v.wait_ge(c_on, u + 2)
                for eo in (0, 1):
                    ch(v.tensor_tensor(on[:, eo], on[:, eo], sg[:, p, eo], ALU.mult))
                for eo in (0, 1):
                    ch.wait(ch.n - 1)
                    ch(v.tensor_copy(oh[:, 2 * p + eo], on[:, eo]))
                ch.wait(ch.n - 1)
                v.tensor_tensor(ol[:, 2 * p], on[:, 0], oh[:, 2 * p], ALU.subtract)
                ch.wait()
                v.tensor_tensor(ol[:, 2 * p + 1], on[:, 1], oh[:, 2 * p + 1], ALU.subtract).then_inc(c_norm, 1)

            def normalise_unit(c, p):
                u = PAIRS * c + p
                v.wait_ge(c_root, u + 2)
                v.wait_ge(c_ev, KINDS * (u + 1) + 3)
                for eo in (0, 1):
                    last = v.scalar_tensor_tensor(on[:, eo], res[:, p, eo], rms_sb[:, eo:eo + 1], bank[5][:, :], ALU.mult, ALU.mult)
                last.then_inc(c_on, 1)

            def gate_low(c, p):
                v.wait_ge(c_oh, PAIRS * c + p + 1)
                v.tensor_tensor(ol[:, 2 * p], on[:, 0], oh[:, 2 * p], ALU.subtract)
                v.tensor_tensor(ol[:, 2 * p + 1], on[:, 1], oh[:, 2 * p + 1], ALU.subtract).then_inc(c_norm, 1)

            def chunk(c, first, last):
                def halves_left():
                    if not first:
                        sigmoids_low(c)
                        gate_low(c - 1, 1)

                angles(c, 0, halves_left)
                recur(c, 0)
                if first:
                    angles(c, 1)
                else:
                    normalise_unit(c - 1, 2)
                    angles(c, 1, lambda: gate_low(c - 1, 2))
                recur(c, 1)
                if last:
                    group_stats(1, 0)
                    group_stats(1, 1)
                else:
                    chunk_stats(c + 1)
                normalise_unit(c, 0)
                angles(c, 2, lambda: gate_low(c, 0))
                if not last:
                    chunk_low(c + 1)
                recur(c, 2)
                if not last:
                    sigmoids(c + 1)
                if last:
                    gate(c, 1)
                else:
                    normalise_unit(c, 1)
                if last:
                    group_stats(1, 2)

            for s, n in ((m_xl, 2), (m_zb, 2), (m_hl, 2), (m_yo, 2), (a_lo, 1),
                         (c_conv, 3), (c_norm, 3), (c_on, 1), (c_scan, 1)):
                v.sem_inc(s, n)
            for g in range(NCH):
                group_stats(0, g)
            for e in range(OWN):
                split_low(e)
            v.wait_ge(consts, 1)
            v.wait_ge(params, 16 * 5)
            ch(v.tensor_copy(lane16[:, :], lane[:, :]))
            ch(v.tensor_copy(tokid16[:, :], tokid[:, :]))
            route(0)
            for p in range(PAIRS):
                for kind in (0, 1):
                    ch(v.tensor_scalar(cang[:, p, kind], conv_sb[:, p, kind], turns_sb[:, kind:kind + 1], None, ALU.mult))
            slots(0)
            for par in (0, 1):
                v.wait_ge(m_yst[par], 16 * (SLOT_TILES // 2 + 1 - par) + 1)
            v.wait_ge(w_save, 16 * E)
            v.memset(raw[:, :, :, 0:HALO], 0.0)
            v.memset(carry, 0.0)
            seq(v.memset(sigab, 0.0))
            chunk_stats(0)
            chunk_low(0)
            sigmoids(0)
            sigmoids_low(0)
            chunk(0, True, False)
            ch.loop(1, NCH - 1, CHUNK_STEPS, lambda c: chunk(c, False, False))
            chunk(NCH - 1, False, True)
            gate(NCH - 1, 2)
            group_stats(1, 3, True)
            route(1)
            slots(1)
            for g in range(NCH):
                if g < NCH - 1:
                    v.wait_ge(g_in[g], 16 * 3)
                combine(g, rows_last[g], yg_last[:, TPC * g:TPC * (g + 1)],
                        lambda i: v.wait_ge(yl_in[TPC * g + i], 32), f_comb)


def kernel(**inputs):
    import concourse.bacc as bacc
    from concourse.bass_utils import run_bass_kernel_spmd as run

    def given(name):
        return np.asarray(inputs["L0_" + name])

    w1 = given("ffn_w1").transpose(2, 0, 1).reshape(KD, P, E, HID).transpose(2, 1, 0, 3).reshape(E, P, KD * HID)
    w2 = np.zeros((E, KH * P, D), np.float32)
    w2[:, 0:HID] = given("ffn_w2").transpose(0, 2, 1)
    w2[:, HID] = given("ffn_b2")
    w2 = w2.reshape(E, KH, P, D).transpose(0, 2, 1, 3).reshape(E, P, KH * D)

    def pairs(w, eo):
        return w[:, eo::2].reshape(w.shape[0], PAIRS, 1, P)

    wq, wk, wv, wg = (given("attn_" + n) for n in ("Wq", "Wk", "Wv", "Wg"))
    cols = np.concatenate([pairs(wq, 0), pairs(wk, 0), pairs(wv, 0), pairs(wv, 1), pairs(wg, 0), pairs(wg, 1)], 2)
    ab = np.concatenate([given("attn_Wa"), given("attn_Wb")], 1)
    wo = given("attn_Wo").reshape(PAIRS, P, 2, D).transpose(1, 0, 2, 3)
    blocks = np.concatenate([cols.reshape(KD, P, NCOL).transpose(1, 0, 2).reshape(P, -1), wo.reshape(P, -1)], 1)
    att_w = np.zeros((PIECES, P, PIECE), np.float32)
    att_w[:, :, :BLOCK] = blocks.reshape(P, PIECES, BLOCK).transpose(1, 0, 2)
    att_w[:KD, :, BLOCK:] = ab.reshape(KD, P, NAB)
    cq, ck, cv = (given("attn_conv_" + n).reshape(PAIRS, P, 2, TAPS) for n in "qkv")
    conv = np.stack([cq[:, :, 0], ck[:, :, 0], cv[:, :, 0], cv[:, :, 1]], 2).transpose(1, 0, 2, 3)
    rms = given("attn_rms_w").reshape(64, 2)
    freq = 1.0 / 10000.0 ** (np.arange(0, P, 2, dtype=np.float32) / P)
    turn = np.tile(freq / (2 * np.pi), 2)
    arrays = {
        "x_in": given("attn_hidden_states").reshape(T, D),
        "ffn_w": np.concatenate([w1, w2], 2),
        "gate_wT": given("ffn_gate_w").T,
        "gate_bias": np.stack([given("ffn_gate_b"), given("ffn_bias")]),
        "b1": given("ffn_b1").reshape(E * HID),
        "att_w": att_w,
        "conv": conv,
        "rms_w": np.concatenate([rms, rms]),
        "turns": np.stack([-turn, turn], 1).astype(np.float32),
    }
    arrays = {k: np.ascontiguousarray(a) for k, a in arrays.items()}
    nc = bacc.Bacc("TRN2", target_bir_lowering=False, num_devices=1)
    args = [nc.dram_tensor(k, a.shape, mybir.dt.from_np(a.dtype), kind="ExternalInput").ap() for k, a in arrays.items()]
    out = nc.dram_tensor("out", (T, D), F32, kind="ExternalOutput").ap()
    build(nc, *args, out)
    r = run(nc, [arrays], core_ids=[0])
    return r.results[0]["out"].reshape(1, T, D)
```
